# Optimizing a Trainium2 kernel written in Bass

```python
import numpy as np
import jax
import jax.numpy as jnp

def _softmax(x, axis=-1):
    return jax.nn.softmax(x, axis=axis)

def _gelu(x):
    return jax.nn.gelu(x, approximate=True)

def _silu(x):
    return jax.nn.silu(x)

def _sigmoid(x):
    return jax.nn.sigmoid(x)

def _layernorm(x, axis=-1, eps=1e-05):
    m = jnp.mean(x, axis=axis, keepdims=True)
    v = jnp.var(x, axis=axis, keepdims=True)
    return (x - m) / jnp.sqrt(v + eps)

def _scatter_add(tgt, idx, src, axis=0):
    return tgt.at[idx].add(src)

def _segment_sum(src, seg, n):
    return jax.ops.segment_sum(src, seg, n)
kernel_name = 'mk_xattn_ffn_d1_seqx_r2_3377ed'

def setup_inputs(seed: int=0):
    np.random.seed(seed)
    _w = jnp.asarray

    def _rec_inputs():
        import jax
        import jax.numpy as jnp
        _rk = jax.random.key(seed)
        x = -0.0005207 + 1.001 * jax.random.normal(jax.random.fold_in(_rk, 1), (8, 1024, 512), jnp.float32)
        _lenS = 1024 - jax.random.randint(jax.random.fold_in(_rk, 7), (8,), 0, max(1, 1024 // 4) + 1, jnp.int32)
        _lenS2 = 1024 - jax.random.randint(jax.random.fold_in(_rk, 8), (8,), 0, max(1, 1024 // 4) + 1, jnp.int32)
        _ctx_1024P = jax.random.normal(jax.random.fold_in(_rk, 11), (8, 16, 512), jnp.float32)
        _ctx_1024c = jax.random.dirichlet(jax.random.fold_in(_rk, 511), 0.3 * jnp.ones((16,), jnp.float32), (8, 1024))
        _ctx_1024t = jnp.einsum('bsk,bkd->bsd', _ctx_1024c, _ctx_1024P)
        _ctx_1024t = _ctx_1024t * jax.lax.rsqrt(jnp.mean(jnp.square(_ctx_1024t)) + 1e-12) * 0.953939
        ctx_1024 = 2.81802e-05 + 1.00001 * (_ctx_1024t + 0.3 * jax.random.normal(jax.random.fold_in(_rk, 611), (8, 1024, 512), jnp.float32))
        _validS = jnp.arange(1024)[None, :] < _lenS[:, None]
        _validS2 = jnp.arange(1024)[None, :] < _lenS2[:, None]
        _causal = jnp.tril(jnp.ones((1024, 1024), dtype=bool))
        mask_Bx1x1xS2_bf1 = jnp.ones((8, 1, 1, 1024), dtype=bool)
        return (x, ctx_1024, mask_Bx1x1xS2_bf1)
    x, ctx_1024, mask_Bx1x1xS2_bf1 = _rec_inputs()

    def _L0_xattn_setup():
        import jax, jax.numpy as jnp
        import numpy as np
        D_MODEL = 512
        N_HEADS = 16
        D_HEAD = D_MODEL // N_HEADS

        def _split_heads(x):
            B, L, D = x.shape
            return x.reshape(B, L, N_HEADS, D_HEAD).transpose(0, 2, 1, 3)
        key = jax.random.key(seed)
        ks = jax.random.split(key, 6)
        B, LQ, LK = (4, 256, 2048)
        scale = 1.0 / np.sqrt(D_MODEL)
        return {'q_in': jax.random.normal(ks[0], (B, LQ, D_MODEL), dtype=jnp.float32), 'mem': jax.random.normal(ks[1], (B, LK, D_MODEL), dtype=jnp.float32), 'mem_mask': jnp.ones((B, 1, 1, LK), dtype=bool), 'Wq': jax.random.normal(ks[2], (D_MODEL, D_MODEL), dtype=jnp.float32) * scale, 'Wk': jax.random.normal(ks[3], (D_MODEL, D_MODEL), dtype=jnp.float32) * scale, 'Wv': jax.random.normal(ks[4], (D_MODEL, D_MODEL), dtype=jnp.float32) * scale, 'Wo': jax.random.normal(ks[5], (D_MODEL, D_MODEL), dtype=jnp.float32) * scale}
    _L0_xattn_all = _L0_xattn_setup()
    _L0_xattn_in = {k: v for k, v in _L0_xattn_all.items() if k in ('Wq', 'Wk', 'Wv', 'Wo')}
    del _L0_xattn_all

    def _L0_ffn_setup():
        import jax, jax.numpy as jnp
        import numpy as np
        DIM = 512

        def _reference_tuple_inner(x, W_r, W_k, W_v, mu_r, mu_k):
            B, T, C = x.shape
            x_prev = jnp.concatenate([jnp.zeros((B, 1, C), x.dtype), x[:, :-1, :]], axis=1)
            xr = mu_r * x + (1.0 - mu_r) * x_prev
            xk = mu_k * x + (1.0 - mu_k) * x_prev
            r = jax.nn.sigmoid(jnp.einsum('btc,dc->btd', xr, W_r))
            k = jnp.einsum('btc,dc->btd', xk, W_k)
            k_act = jnp.square(jax.nn.relu(k))
            out = r * jnp.einsum('btc,dc->btd', k_act, W_v)
            new_state = x[:, -1, :]
            return (out, new_state)
        key = jax.random.key(seed)
        ks = jax.random.split(key, 6)
        B, T, C = (8, 1024, DIM)
        x = jax.random.normal(ks[0], (B, T, C), dtype=jnp.float32)
        s = 1.0 / np.sqrt(C)
        W_r = jax.random.uniform(ks[1], (C, C), jnp.float32, -s, s)
        W_k = jax.random.uniform(ks[2], (C, C), jnp.float32, -s, s)
        W_v = jax.random.uniform(ks[3], (C, C), jnp.float32, -s, s)
        mu_r = jax.random.uniform(ks[4], (C,), jnp.float32)
        mu_k = jax.random.uniform(ks[5], (C,), jnp.float32)
        return {'x': x, 'W_r': W_r, 'W_k': W_k, 'W_v': W_v, 'mu_r': mu_r, 'mu_k': mu_k}
    _L0_ffn_all = _L0_ffn_setup()
    _L0_ffn_in = {k: v for k, v in _L0_ffn_all.items() if k in ('W_r', 'W_k', 'W_v', 'mu_r', 'mu_k')}
    del _L0_ffn_all
    return {'x': x, 'ctx_1024': ctx_1024, 'mask_Bx1x1xS2_bf1': mask_Bx1x1xS2_bf1, 'L0_xattn_Wq': _L0_xattn_in['Wq'], 'L0_xattn_Wk': _L0_xattn_in['Wk'], 'L0_xattn_Wv': _L0_xattn_in['Wv'], 'L0_xattn_Wo': _L0_xattn_in['Wo'], 'L0_ffn_W_r': _L0_ffn_in['W_r'], 'L0_ffn_W_k': _L0_ffn_in['W_k'], 'L0_ffn_W_v': _L0_ffn_in['W_v'], 'L0_ffn_mu_r': _L0_ffn_in['mu_r'], 'L0_ffn_mu_k': _L0_ffn_in['mu_k']}

def reference(x, ctx_1024, mask_Bx1x1xS2_bf1, L0_xattn_Wq, L0_xattn_Wk, L0_xattn_Wv, L0_xattn_Wo, L0_ffn_W_r, L0_ffn_W_k, L0_ffn_W_v, L0_ffn_mu_r, L0_ffn_mu_k):
    import jax
    import jax.numpy as jnp

    def _L0_xattn_ref(q_in, mem, mem_mask, Wq, Wk, Wv, Wo):
        import jax, jax.numpy as jnp
        import numpy as np
        D_MODEL = 512
        N_HEADS = 16
        D_HEAD = D_MODEL // N_HEADS

        def _split_heads(x):
            B, L, D = x.shape
            return x.reshape(B, L, N_HEADS, D_HEAD).transpose(0, 2, 1, 3)
        q = _split_heads(q_in @ Wq.T)
        k = _split_heads(mem @ Wk.T)
        v = _split_heads(mem @ Wv.T)
        scores = jnp.einsum('bhqd,bhkd->bhqk', q, k) / jnp.sqrt(jnp.float32(D_HEAD))
        scores = jnp.where(mem_mask, scores, -jnp.inf)
        attn = jax.nn.softmax(scores, axis=-1)
        out = jnp.einsum('bhqk,bhkd->bhqd', attn, v)
        B, H, LQ, Dh = out.shape
        out = out.transpose(0, 2, 1, 3).reshape(B, LQ, H * Dh)
        return out @ Wo.T

    def _L0_ffn_ref(x, W_r, W_k, W_v, mu_r, mu_k):
        import jax, jax.numpy as jnp
        import numpy as np
        DIM = 512

        def _reference_tuple_inner(x, W_r, W_k, W_v, mu_r, mu_k):
            B, T, C = x.shape
            x_prev = jnp.concatenate([jnp.zeros((B, 1, C), x.dtype), x[:, :-1, :]], axis=1)
            xr = mu_r * x + (1.0 - mu_r) * x_prev
            xk = mu_k * x + (1.0 - mu_k) * x_prev
            r = jax.nn.sigmoid(jnp.einsum('btc,dc->btd', xr, W_r))
            k = jnp.einsum('btc,dc->btd', xk, W_k)
            k_act = jnp.square(jax.nn.relu(k))
            out = r * jnp.einsum('btc,dc->btd', k_act, W_v)
            new_state = x[:, -1, :]
            return (out, new_state)
        return _reference_tuple_inner(x, W_r, W_k, W_v, mu_r, mu_k)[0]
    x = x + _L0_xattn_ref(_layernorm(x, axis=-1), ctx_1024, mask_Bx1x1xS2_bf1, L0_xattn_Wq, L0_xattn_Wk, L0_xattn_Wv, L0_xattn_Wo)
    x = x + _L0_ffn_ref(_layernorm(x, axis=-1), L0_ffn_W_r, L0_ffn_W_k, L0_ffn_W_v, L0_ffn_mu_r, L0_ffn_mu_k)
    return x

_drawn_inputs = setup_inputs


def setup_inputs(seed=0):
    import zlib

    import numpy as np

    out = dict(_drawn_inputs(seed))
    spreads = {}
    factors = {'L0_ffn_W_r': 3.132, 'L0_ffn_mu_r': 7.492}
    for name, (base, spread) in spreads.items():
        noise = np.random.default_rng([zlib.crc32(name.encode()), seed]).standard_normal(out[name].shape)
        drawn = base * np.exp(spread * noise) if base else spread * noise
        out[name] = jnp.asarray(drawn.astype(out[name].dtype))
    for name, factor in factors.items():
        out[name] = (out[name] * factor).astype(out[name].dtype)
    return out
```

```python
from contextlib import ExitStack

import concourse.bass as bass
from concourse import mybir
from concourse.alu_op_type import AluOpType as ALU

F32 = mybir.dt.float32
F32R = mybir.dt.float32r
U8 = mybir.dt.uint8
ACT = mybir.ActivationFunctionType

B, L, D = 8, 1024, 512
H, DH = 16, 32
P = 128
C = D // P
BLK = 512
NB = L // BLK
TT = BLK // P
HG = P // DH
G = H // HG
QT = L // P
KC = L // P
NG = B * G
STACK = 3 * DH + 1
EPS = 1e-5
SCALE = float(1.0 / DH ** 0.5)
MASKED = float(2.0 ** 120)


def products(nc, out, stat, mov):
    n = 0
    for c in range(C):
        for s, m in ((1, 0), (0, 1), (0, 0)):
            last = nc.tensor.matmul(out, stat(s, c), mov(m, c), start=n == 0, stop=n == 3 * C - 1)
            n += 1
    return last


def make_identity(nc, ident, made):
    nc.gpsimd.memset(ident[:], 0.0).then_inc(made, 1)
    nc.gpsimd.wait_ge(made, 1)
    nc.gpsimd.affine_select(out=ident[:], in_=ident[:], compare_op=ALU.not_equal, fill=1.0, base=0,
                            pattern=[[-1, P]], channel_multiplier=1).then_inc(made, 1)


def prepare_weights(nc, tag, weights, halves, ident, identity_made, first, mask=None, mask_rows=None):
    with ExitStack() as ctx:
        nat = [ctx.enter_context(nc.sbuf_tensor(f"{tag}_nat{k}", [P, C, D], F32)) for k in range(len(weights))]
        banks = [ctx.enter_context(nc.psum_tensor(f"{tag}_bank{k}", [P, D], F32)) for k in range(4)]
        loaded = [ctx.enter_context(nc.semaphore(f"{tag}_loaded{k}")) for k in range(len(weights))]
        transposed = ctx.enter_context(nc.semaphore(f"{tag}_transposed"))
        high_made = ctx.enter_context(nc.semaphore(f"{tag}_high"))
        low_made = ctx.enter_context(nc.semaphore(f"{tag}_low"))
        if mask is not None:
            mask_in = ctx.enter_context(nc.sbuf_tensor("mask_in", [B, L], U8))
            mask_row = ctx.enter_context(nc.sbuf_tensor("mask_row", [B, L], F32R))
            mask_loaded = ctx.enter_context(nc.semaphore("mask_loaded"))
            mask_made = ctx.enter_context(nc.semaphore("mask_made"))
            mask_stored = ctx.enter_context(nc.semaphore("mask_stored"))
        block = ctx.enter_context(nc.Block())

        @block.sync
        def _(sp):
            for k, w in enumerate(weights):
                sp.dma_start(nat[k][:], w.rearrange("(o p) c -> p o c", p=P)).then_inc(loaded[k], 16)
            if mask is not None:
                sp.dma_start(mask_in[:], mask.rearrange("b x y k -> (b x y) k")).then_inc(mask_loaded, 16)
                sp.wait_ge(mask_made, 1)
                for g in range(G):
                    sp.dma_start(mask_rows.rearrange("(b g) k -> g b k", g=G)[g],
                                 mask_row[:].bitcast(F32)).then_inc(mask_stored, 16)
                sp.wait_ge(mask_stored, 16 * G)

        @block.gpsimd
        def _(pool):
            if first:
                make_identity(nc, ident, identity_made)

        @block.tensor
        def _(pe):
            pe.wait_ge(identity_made, 2)
            for k in range(len(weights)):
                pe.wait_ge(loaded[k], 16)
                for c in range(C):
                    n = k * C + c
                    if n >= 4:
                        pe.wait_ge(low_made, n - 3)
                    for o in range(C):
                        last = nc.tensor.transpose(banks[n % 4][:, o * P:(o + 1) * P],
                                                   nat[k][:, o, c * P:(c + 1) * P], ident[:])
                    last.then_inc(transposed, 1)

        @block.scalar
        def _(act):
            for k in range(len(weights)):
                for c in range(C):
                    n = k * C + c
                    act.wait_ge(transposed, n + 1)
                    nc.scalar.activation(halves[k][0][:, c, :], banks[n % 4][:], ACT.Copy).then_inc(high_made, 1)

        @block.vector
        def _(dve):
            for k in range(len(weights)):
                for c in range(C):
                    n = k * C + c
                    dve.wait_ge(high_made, n + 1)
                    nc.vector.tensor_tensor(halves[k][1][:, c, :], banks[n % 4][:],
                                            halves[k][0][:, c, :].bitcast(F32), ALU.subtract).then_inc(low_made, 1)
            if mask is not None:
                dve.wait_ge(mask_loaded, 16)
                nc.vector.tensor_scalar(mask_row[:], mask_in[:], MASKED, -MASKED, ALU.mult, ALU.add).then_inc(mask_made, 1)


def project(nc, x, ctx_in, wq, wk, wv, ident, q_half, k_half, v_rows, q_scale=SCALE):
    with ExitStack() as ctx:
        def sb(name, shape, dt=F32):
            return ctx.enter_context(nc.sbuf_tensor("a_" + name, shape, dt))

        def sem(name):
            return ctx.enter_context(nc.semaphore("a_" + name))

        x_in = [sb(f"x_in{j}", [P, TT, D]) for j in range(NB)]
        c_in = [sb(f"c_in{j}", [P, TT, D]) for j in range(NB)]
        xT = [sb(f"xT{s}", [P, C, BLK], F32R) for s in range(2)]
        cT = [sb(f"cT{s}", [P, C, BLK], F32R) for s in range(2)]
        q_out = [sb(f"q_out{s}", [P, C, BLK], F32R) for s in range(2)]
        k_out = [sb(f"k_out{s}", [P, C, BLK], F32R) for s in range(2)]
        v_out = sb("v_out", [P, TT, D])
        stats = sb("stats", [P, TT, 6])
        moments = sb("moments", [P, TT, 2])
        power = sb("power", [P, TT])
        variance = sb("variance", [P, TT])
        rstd = sb("rstd", [P, TT])
        t_bank = [ctx.enter_context(nc.psum_tensor(f"a_t{k}", [P, BLK], F32)) for k in range(2)]
        p_bank = [ctx.enter_context(nc.psum_tensor(f"a_p{k}", [P, BLK], F32)) for k in range(6)]
        x_loaded = [sem(f"x_loaded{j}") for j in range(NB)]
        c_loaded = [sem(f"c_loaded{j}") for j in range(NB)]
        PB = 3 * C
        power_made = sem("power_made")
        stats_made = sem("stats_made")
        stats_seen = sem("stats_seen")
        moments_made = sem("moments_made")
        variance_made = sem("variance_made")
        rstd_made = sem("rstd_made")
        normalised = sem("normalised")
        x_turned = sem("x_turned")
        c_turned = sem("c_turned")
        turned_high = sem("turned_high")
        t_free = sem("t_free")
        projected = sem("projected")
        out_high = sem("out_high")
        bank_free = sem("bank_free")
        q_stored = sem("q_stored")
        k_stored = sem("k_stored")
        v_stored = sem("v_stored")
        block = ctx.enter_context(nc.Block())

        @block.sync
        def _(sp):
            def load_x(i, j):
                sp.dma_start(x_in[j][:], x[i, j * BLK:(j + 1) * BLK, :].rearrange("(t p) c -> p t c", p=P)
                             ).then_inc(x_loaded[j], 16)

            def load_c(i, j):
                sp.dma_start(c_in[j][:], ctx_in[i, j * BLK:(j + 1) * BLK, :].rearrange("(t p) c -> p t c", p=P)
                             ).then_inc(c_loaded[j], 16)

            def store(i, j):
                n = NB * i + j
                for first, out, half, stored in ((0, q_out, q_half, q_stored), (C, k_out, k_half, k_stored)):
                    sp.wait_ge(bank_free, n * PB + (6 + first + C))
                    for s in range(2):
                        sp.dma_start(half[s][i, :, :, j * BLK:(j + 1) * BLK], out[s][:].bitcast(F32)
                                     ).then_inc(stored, 16)
                sp.wait_ge(bank_free, n * PB + (6 + PB))
                for g in range(G):
                    sp.dma_start(v_rows[i, g, :, j * TT:(j + 1) * TT, :], v_out[:, :, g * P:(g + 1) * P]
                                 ).then_inc(v_stored, 16)

            for j in range(NB):
                load_x(0, j)
                load_c(0, j)
            with sp.Fori(0, B - 1) as i:
                for j in range(NB):
                    sp.wait_ge(c_turned, (NB * i + j) * C + C)
                    load_c(i + 1, j)
                    sp.wait_ge(x_turned, (NB * i + j) * C + C)
                    load_x(i + 1, j)
                    store(i, j)
            for j in range(NB):
                store(B - 1, j)
            sp.wait_ge(q_stored, 32 * (NB * B + 1))
            sp.wait_ge(k_stored, 32 * (NB * B + 1))
            sp.wait_ge(v_stored, 16 * G * (NB * B + 1))

        @block.tensor
        def _(pe):
            def turn(src, i, j, before, turned):
                for c in range(C):
                    pe.wait_ge(t_free, (NB * i + j) * 2 * C + (before + c + 1))
                    for tt in range(TT):
                        last = nc.tensor.transpose(t_bank[c % 2][:, tt * P:(tt + 1) * P],
                                                   src[:, tt, c * P:(c + 1) * P], ident[:])
                    last.then_inc(turned, 1)

            def turn_x(i, j):
                pe.wait_ge(normalised, (NB * i + j) + 1)
                turn(x_in[j], i, j, 0, x_turned)

            def turn_c(i, j):
                pe.wait_ge(c_loaded[j], i * 16 + 16)
                turn(c_in[j], i, j, C, c_turned)

            def stage(i, j, ahead):
                n = NB * i + j
                turn_c(i, j)
                for first, w, src in ((0, wq, xT), (C, wk, cT)):
                    pe.wait_ge(t_free, n * 2 * C + (2 + C + first))
                    for o in range(C):
                        pe.wait_ge(bank_free, n * PB + (first + o + 1))
                        products(nc, p_bank[(first + o) % 6][:], lambda s, c: w[s][:, c, o * P:(o + 1) * P],
                                 lambda s, c: src[s][:, c, :]).then_inc(projected, 1)
                if ahead:
                    turn_x(*ahead)
                for tt in range(TT):
                    pe.wait_ge(bank_free, n * PB + (2 * C + tt + 1))
                    products(nc, p_bank[(2 * C + tt) % 6][:], lambda s, c: cT[s][:, c, tt * P:(tt + 1) * P],
                             lambda s, c: wv[s][:, c, :]).then_inc(projected, 1)

            turn_x(0, 0)
            with pe.Fori(0, B - 1) as i:
                stage(i, 0, (i, 1))
                stage(i, 1, (i + 1, 0))
            stage(B - 1, 0, (B - 1, 1))
            stage(B - 1, 1, None)

        @block.gpsimd
        def _(pool):
            nc.gpsimd.memset(power[:], -0.5).then_inc(power_made, 1)
            pool.wait_ge(power_made, 1)
            with pool.Fori(0, NB * B) as n:
                pool.wait_ge(variance_made, n + 1)
                nc.gpsimd.tensor_tensor(rstd[:], variance[:], power[:], ALU.pow).then_inc(rstd_made, 1)

        @block.scalar
        def _(act):
            act.sem_inc(q_stored, 32)
            act.sem_inc(k_stored, 32)

            def split_high(i, j, dst, turned):
                for c in range(C):
                    act.wait_ge(turned, (NB * i + j) * C + (c + 1))
                    nc.scalar.activation(dst[:, c, :], t_bank[c % 2][:], ACT.Copy).then_inc(turned_high, 1)

            def stage(i, j, ahead):
                n = NB * i + j
                split_high(i, j, cT[0], c_turned)
                for out, stored, first, scale in ((q_out, q_stored, 0, SCALE), (k_out, k_stored, C, 1.0)):
                    act.wait_ge(stored, n * 32 + 32)
                    for o in range(C):
                        act.wait_ge(projected, n * PB + (first + o + 1))
                        nc.scalar.activation(out[0][:, o, :], p_bank[(first + o) % 6][:], ACT.Copy, scale=scale
                                             ).then_inc(out_high, 1)
                if ahead:
                    split_high(*ahead, xT[0], x_turned)

            split_high(0, 0, xT[0], x_turned)
            with act.Fori(0, B - 1) as i:
                stage(i, 0, (i, 1))
                stage(i, 1, (i + 1, 0))
            stage(B - 1, 0, (B - 1, 1))
            stage(B - 1, 1, None)

        @block.vector
        def _(dve):
            dve.sem_inc(t_free, 2)
            dve.sem_inc(bank_free, 6)
            dve.sem_inc(v_stored, 16 * G)

            def moments_of(i, j):
                n = NB * i + j
                dve.wait_ge(x_loaded[j], i * 16 + 16)
                for tt in range(TT):
                    last = nc.vector.bn_stats(stats[:, tt, :], x_in[j][:, tt, :])
                last.then_inc(stats_made, 1)
                dve.wait_ge(stats_made, n + 1)
                dve.sem_inc(stats_seen, 1)
                for tt in range(TT):
                    last = nc.vector.bn_aggr(moments[:, tt, :], stats[:, tt, :])
                last.then_inc(moments_made, 1)
                dve.wait_ge(moments_made, n + 1)
                nc.vector.tensor_scalar(variance[:], moments[:, :, 1], EPS, None, ALU.add).then_inc(variance_made, 1)

            def normalise(i, j):
                dve.wait_ge(rstd_made, (NB * i + j) + 1)
                for tt in range(TT):
                    last = nc.vector.tensor_scalar(x_in[j][:, tt, :], x_in[j][:, tt, :], moments[:, tt, 0:1],
                                                   rstd[:, tt:tt + 1], ALU.subtract, ALU.mult)
                last.then_inc(normalised, 1)

            def split_low(i, j, before, dst):
                for c in range(C):
                    dve.wait_ge(turned_high, (NB * i + j) * 2 * C + (before + c + 1))
                    nc.vector.tensor_tensor(dst[1][:, c, :], t_bank[c % 2][:], dst[0][:, c, :].bitcast(F32),
                                            ALU.subtract).then_inc(t_free, 1)

            def stage(i, j, ahead):
                n = NB * i + j
                split_low(i, j, C, cT)
                if ahead:
                    moments_of(*ahead)
                for out, first, scale in ((q_out, 0, SCALE), (k_out, C, 1.0)):
                    for o in range(C):
                        dve.wait_ge(out_high, n * 2 * C + (first + o + 1))
                        nc.vector.scalar_tensor_tensor(out[1][:, o, :], p_bank[(first + o) % 6][:], scale,
                                                       out[0][:, o, :].bitcast(F32), ALU.mult, ALU.subtract
                                                       ).then_inc(bank_free, 1)
                    if ahead and first == 0:
                        normalise(*ahead)
                if ahead:
                    split_low(*ahead, 0, xT)
                dve.wait_ge(v_stored, n * (16 * G) + 16 * G)
                for tt in range(TT):
                    dve.wait_ge(projected, n * PB + (2 * C + tt + 1))
                    nc.vector.tensor_copy(v_out[:, tt, :], p_bank[(2 * C + tt) % 6][:]).then_inc(bank_free, 1)

            moments_of(0, 0)
            normalise(0, 0)
            split_low(0, 0, 0, xT)
            with dve.Fori(0, B - 1) as i:
                stage(i, 0, (i, 1))
                stage(i, 1, (i + 1, 0))
            stage(B - 1, 0, (B - 1, 1))
            stage(B - 1, 1, None)

def attend(nc, q_half, k_half, v_rows, mask_rows, ident, attended):
    with ExitStack() as ctx:
        def sb(name, shape, dt=F32):
            return ctx.enter_context(nc.sbuf_tensor("b_" + name, shape, dt))

        def sem(name):
            return ctx.enter_context(nc.semaphore("b_" + name))

        NP = 3
        UG = QT * HG
        q_stack = [sb(f"q_stack{p}", [STACK, HG, L], F32R) for p in range(2)]
        k_stack = [sb(f"k_stack{p}", [STACK, HG, L], F32R) for p in range(2)]
        v_in = [sb(f"v_in{p}", [P, KC, P]) for p in range(2)]
        ones = sb("ones", [1, L])
        prob = [sb(f"prob{k}", [P, L]) for k in range(NP)]
        prob_t = [sb(f"prob_t{k}", [P, HG, KC, P]) for k in range(2)]
        neg_max = sb("neg_max", [P, 4])
        total = sb("total", [P, 2, HG])
        inverse = sb("inverse", [P, 2, HG])
        ones_wide = sb("ones_wide", [P, P])
        inverse_wide = sb("inverse_wide", [P, HG, DH])
        spread = sb("spread", [P, P])
        result = [sb(f"result{p}", [P, L]) for p in range(2)]
        score = [ctx.enter_context(nc.psum_tensor(f"b_score{k}", [P, L], F32)) for k in range(2)]
        turn_bank = [ctx.enter_context(nc.psum_tensor(f"b_turn{k}", [P, 4, P], F32)) for k in range(2)]
        out_bank = ctx.enter_context(nc.psum_tensor("b_out_bank", [P, 4, P], F32))[:, 0, :]
        spread_bank = ctx.enter_context(nc.psum_tensor("b_spread_bank", [P, 4, P], F32))[:, 0, :]
        stacks_loaded = [sem(f"stacks_loaded{p}") for p in range(2)]
        ones_made = sem("ones_made")
        ones_set = sem("ones_set")
        scored = sem("scored")
        max_made = sem("max_made")
        exp_made = sem("exp_made")
        turned = [sem(f"turned{k}") for k in range(2)]
        turn_read = [sem(f"turn_read{k}") for k in range(2)]
        inverse_made = sem("inverse_made")
        ones_wide_made = sem("ones_wide_made")
        widened = sem("widened")
        spread_turned = sem("spread_turned")
        spread_made = sem("spread_made")
        gathered = sem("gathered")
        result_made = sem("result_made")
        stored = [sem(f"stored{p}") for p in range(2)]
        block = ctx.enter_context(nc.Block())

        DMAS = 6 + HG + 1

        @block.sync
        def _(sp):
            def load(i, p):
                g = 2 * i + p
                for r, half in enumerate((0, 0, 1)):
                    sp.dma_start(q_stack[p][r * DH:(r + 1) * DH, :, :].bitcast(F32),
                                 q_half[half][g].rearrange("(h d) t -> d h t", d=DH)).then_inc(stacks_loaded[p], 16)
                for r, half in enumerate((0, 1, 0)):
                    sp.dma_start(k_stack[p][r * DH:(r + 1) * DH, :, :].bitcast(F32),
                                 k_half[half][g].rearrange("(h d) t -> d h t", d=DH)).then_inc(stacks_loaded[p], 16)
                for h in range(HG):
                    sp.dma_start(k_stack[p][STACK - 1:STACK, h, :].bitcast(F32), mask_rows[g].rearrange("(a k) -> a k", a=1)
                                 ).then_inc(stacks_loaded[p], 16)
                sp.dma_start(v_in[p][:], v_rows[g]).then_inc(stacks_loaded[p], 16)

            def store(i, p):
                g = 2 * i + p
                sp.wait_ge(result_made, g * QT + (QT + 2))
                sp.dma_start(attended[g], result[p][:]).then_inc(stored[p], 16)

            sp.wait_ge(ones_made, 1)
            for p in range(2):
                for h in range(HG):
                    sp.dma_start(q_stack[p][STACK - 1:STACK, h, :].bitcast(F32), ones[:]).then_inc(ones_set, 16)
            load(0, 0)
            load(0, 1)
            with sp.Fori(0, NG // 2 - 1) as i:
                for p in range(2):
                    store(i, p)
                    load(i + 1, p)
            store(NG // 2 - 1, 0)
            store(NG // 2 - 1, 1)
            for p in range(2):
                sp.wait_ge(stored[p], 16 * (NG // 2 + 1))

        @block.gpsimd
        def _(pool):
            nc.gpsimd.memset(ones[:], 1.0).then_inc(ones_made, 1)
            nc.gpsimd.memset(ones_wide[:], 1.0).then_inc(ones_wide_made, 1)
            pool.wait_ge(ones_wide_made, 1)

            def widen(n, slot):
                pool.wait_ge(inverse_made, n + (slot + 1))
                if slot:
                    pool.wait_ge(spread_turned, n + slot)
                nc.gpsimd.tensor_tensor(inverse_wide[:], inverse[:, slot % 2, :].unsqueeze(2).broadcast_to([P, HG, DH]),
                                        ones_wide[:].rearrange("p (h d) -> p h d", h=HG), ALU.mult).then_inc(widened, 1)

            widen(0, 0)
            widen(0, 1)
            with pool.Fori(1, NG * QT // 2) as t:
                pool.wait_ge(spread_turned, t * 2)
                widen(t * 2, 0)
                widen(t * 2, 1)

        @block.tensor
        def _(pe):
            def scores(i, p, u):
                g, h = 2 * i + p, u % HG
                if u == 0:
                    pe.wait_ge(stacks_loaded[p], i * (16 * DMAS) + 16 * DMAS)
                for half in range(2):
                    last = nc.tensor.matmul(score[u % 2][:, half * BLK:(half + 1) * BLK],
                                            q_stack[p][:, h, (u // HG) * P:(u // HG + 1) * P],
                                            k_stack[p][:, h, half * BLK:(half + 1) * BLK], start=True, stop=True)
                last.then_inc(scored, 1)

            def turn(i, p, u):
                g = 2 * i + p
                for k in range(2):
                    pe.wait_ge(turn_read[k], g * UG + (u + 1))
                    for c in range(4):
                        kc = 4 * k + c
                        last = nc.tensor.transpose(turn_bank[k][:, c, :], prob[u % NP][:, kc * P:(kc + 1) * P], ident[:])
                    last.then_inc(turned[k], 1)

            def gather(i, p, qt):
                g = 2 * i + p
                pe.wait_ge(widened, g * QT + (qt + 1))
                pe.wait_ge(result_made, g * QT + (qt + 2))
                nc.tensor.transpose(spread_bank, inverse_wide[:].rearrange("p h d -> p (h d)"), ident[:]
                                    ).then_inc(spread_turned, 1)
                for k in range(2):
                    pe.wait_ge(turn_read[k], g * UG + (HG * qt + HG + 1))
                for kc in range(KC):
                    for h in range(HG):
                        last = nc.tensor.matmul(out_bank[h * DH:(h + 1) * DH, :], v_in[p][:, kc, h * DH:(h + 1) * DH],
                                                prob_t[qt % 2][:, h, kc, :], start=kc == 0, stop=kc == KC - 1,
                                                tile_position=(0, h * DH))
                last.then_inc(gathered, 1)

            def pair(i, last):
                for p in range(2):
                    g = 2 * i + p
                    for u in range(UG):
                        pe.wait_ge(exp_made, g * UG + (u + 1))
                        if u + 2 < UG:
                            scores(i, p, u + 2)
                        elif p == 0:
                            scores(i, 1, u + 2 - UG)
                        elif not last:
                            scores(i + 1, 0, u + 2 - UG)
                        turn(i, p, u)
                        if u % HG == 0 and u:
                            gather(i, p, u // HG - 1)
                    gather(i, p, QT - 1)

            pe.wait_ge(ones_set, 32 * HG)
            scores(0, 0, 0)
            scores(0, 0, 1)
            with pe.Fori(0, NG // 2 - 1) as i:
                pair(i, False)
            pair(NG // 2 - 1, True)

        @block.scalar
        def _(act):
            act.sem_inc(turn_read[1], 1)

            def exponentials(i, p, u):
                g = 2 * i + p
                act.wait_ge(max_made, g * UG + (u + 1))
                nc.scalar.activation(prob[u % NP][:], score[u % 2][:], ACT.Exp, bias=neg_max[:, u % 4:u % 4 + 1],
                                     accum_out=total[:, u // HG % 2, u % HG:u % HG + 1]).then_inc(exp_made, 1)

            def copy_turned(i, p, u):
                if u % HG == 0:
                    act.wait_ge(result_made, (2 * i + p) * QT + (u // HG + 1))
                act.wait_ge(turned[1], (2 * i + p) * UG + (u + 1))
                nc.scalar.activation(prob_t[u // HG % 2][:, u % HG, 4:8, :], turn_bank[1][:], ACT.Copy
                                     ).then_inc(turn_read[1], 1)

            def group(i, p):
                for u in range(UG):
                    exponentials(i, p, u)
                    if u:
                        copy_turned(i, p, u - 1)
                    if u % HG == 2 and u > HG:
                        spread_copy(i, p, u // HG - 1)
                copy_turned(i, p, UG - 1)
                spread_copy(i, p, QT - 1)

            def spread_copy(i, p, qt):
                act.wait_ge(result_made, (2 * i + p) * QT + (qt + 2))
                act.wait_ge(spread_turned, (2 * i + p) * QT + (qt + 1))
                nc.scalar.activation(spread[:], spread_bank, ACT.Copy).then_inc(spread_made, 1)

            with act.Fori(0, NG // 2) as i:
                for p in range(2):
                    group(i, p)

        @block.vector
        def _(dve):
            dve.sem_inc(turn_read[0], 1)
            dve.sem_inc(result_made, 2)
            for p in range(2):
                dve.sem_inc(stored[p], 16)

            def maxima(i, p, u):
                dve.wait_ge(scored, (2 * i + p) * UG + (u + 1))
                nc.vector.tensor_reduce(neg_max[:, u % 4:u % 4 + 1], score[u % 2][:], mybir.AxisListType.X, ALU.max,
                                        negate=True).then_inc(max_made, 1)

            def copy_turned(i, p, u):
                dve.wait_ge(turned[0], (2 * i + p) * UG + (u + 1))
                nc.vector.tensor_copy(prob_t[u // HG % 2][:, u % HG, 0:4, :], turn_bank[0][:]).then_inc(turn_read[0], 1)

            def invert(i, p, qt):
                dve.wait_ge(exp_made, (2 * i + p) * UG + (HG * qt + HG))
                nc.vector.reciprocal(inverse[:, qt % 2, :], total[:, qt % 2, :]).then_inc(inverse_made, 1)

            def normalise(i, p, qt):
                n = (2 * i + p) * QT
                dve.wait_ge(gathered, n + (qt + 1))
                dve.wait_ge(spread_made, n + (qt + 1))
                nc.vector.tensor_tensor(result[p][:, qt * P:(qt + 1) * P], out_bank, spread[:], ALU.mult
                                        ).then_inc(result_made, 1)

            def group(i, p):
                dve.wait_ge(stored[p], i * 16 + 16)
                for u in range(UG):
                    maxima(i, p, u)
                    if u:
                        copy_turned(i, p, u - 1)
                    if u % HG == 0 and u:
                        invert(i, p, u // HG - 1)
                    if u % HG == 3 and u > HG:
                        normalise(i, p, u // HG - 1)
                copy_turned(i, p, UG - 1)
                invert(i, p, QT - 1)
                normalise(i, p, QT - 1)

            with dve.Fori(0, NG // 2) as i:
                for p in range(2):
                    group(i, p)


def finish(nc, x, attended, mu, wo, wr, wk, wv, ident, out):
    with ExitStack() as ctx:
        def sb(name, shape, dt=F32):
            return ctx.enter_context(nc.sbuf_tensor("c_" + name, shape, dt))

        def sem(name):
            return ctx.enter_context(nc.semaphore("c_" + name))

        a_in = sb("a_in", [P, G, BLK])
        a_half = [sb(f"a_half{s}", [P, G, BLK], F32R) for s in range(2)]
        x1 = [sb(f"x1_{j}", [P, TT, D]) for j in range(NB)]
        xn = sb("xn", [P, TT, D])
        xT = sb("xT", [P, C, 1 + BLK])
        part = [sb(f"part{c}", [P, BLK]) for c in range(3)]
        mixed = [sb(f"mixed{c}", [P, BLK]) for c in range(C)]
        xk = [sb(f"xk{s}", [P, C, BLK], F32R) for s in range(2)]
        xr = [sb(f"xr{s}", [P, C, BLK], F32R) for s in range(2)]
        act_sq = [sb(f"act_sq{o}", [P, BLK]) for o in range(C)]
        kact = [sb(f"kact{s}", [P, C, BLK], F32R) for s in range(2)]
        gate = sb("gate", [P, TT, D])
        final = sb("final", [P, TT, D])
        mus = [sb(f"mu{k}", [P, C]) for k in range(2)]
        rest = [sb(f"rest{k}", [P, C]) for k in range(2)]
        stats = sb("stats", [P, TT, 6])
        moments = sb("moments", [P, TT, 2])
        variance = sb("variance", [P, TT])
        power = sb("power", [P, TT])
        rstd = sb("rstd", [P, TT])
        t_bank = [ctx.enter_context(nc.psum_tensor(f"c_t{k}", [P, BLK], F32)) for k in range(2)]
        a_bank = [ctx.enter_context(nc.psum_tensor(f"c_a{k}", [P, BLK], F32)) for k in range(2)]
        v_bank = [ctx.enter_context(nc.psum_tensor(f"c_v{k}", [P, BLK], F32)) for k in range(4)]
        mu_loaded = sem("mu_loaded")
        rest_made = sem("rest_made")
        a_loaded = sem("a_loaded")
        x_loaded = [sem(f"x_loaded{j}") for j in range(NB)]
        a_high = sem("a_high")
        a_low = sem("a_low")
        o_done = sem("o_done")
        x1_made = sem("x1_made")
        stats_made = sem("stats_made")
        stats_seen = sem("stats_seen")
        moments_made = sem("moments_made")
        variance_made = sem("variance_made")
        power_made = sem("power_made")
        rstd_made = sem("rstd_made")
        normalised = sem("normalised")
        turned = sem("turned")
        t_free = sem("t_free")
        carried = sem("carried")
        part_made = sem("part_made")
        mix_made = sem("mix_made")
        mix_high = sem("mix_high")
        mix_low = sem("mix_low")
        k_done = sem("k_done")
        r_done = sem("r_done")
        v_done = sem("v_done")
        a_free = sem("a_free")
        v_free = sem("v_free")
        relu_made = sem("relu_made")
        square_made = sem("square_made")
        kact_high = sem("kact_high")
        kact_low = sem("kact_low")
        gate_made = sem("gate_made")
        product_made = sem("product_made")
        final_made = sem("final_made")
        stored = sem("stored")
        block = ctx.enter_context(nc.Block())

        @block.sync
        def _(sp):
            def load_a(i, j):
                sp.dma_start(a_in[:], attended[i, :, :, j * BLK:(j + 1) * BLK].rearrange("g p t -> p g t")
                             ).then_inc(a_loaded, 16)

            def load_x(i, j):
                sp.dma_start(x1[j][:], x[i, j * BLK:(j + 1) * BLK, :].rearrange("(t p) c -> p t c", p=P)
                             ).then_inc(x_loaded[j], 16)

            def stage(i, j, after):
                n = NB * i + j
                if after:
                    sp.wait_ge(a_high, n + 2)
                    sp.wait_ge(a_low, n + 2)
                    load_a(*after)
                sp.wait_ge(final_made, n * TT + 2 * TT)
                sp.dma_start(out[i, j * BLK:(j + 1) * BLK, :].rearrange("(t p) c -> p t c", p=P), final[:]
                             ).then_inc(stored, 16)
                if after:
                    load_x(*after)

            for k in range(2):
                sp.dma_start(mus[k][:], mu[k].rearrange("(c p) -> p c", p=P), allow_slow_non_contiguous=True).then_inc(mu_loaded, 16)
            load_a(0, 0)
            load_x(0, 0)
            load_x(0, 1)
            sp.wait_ge(a_high, 1)
            sp.wait_ge(a_low, 1)
            load_a(0, 1)
            with sp.Fori(0, B - 1) as i:
                stage(i, 0, (i + 1, 0))
                stage(i, 1, (i + 1, 1))
            stage(B - 1, 0, None)
            stage(B - 1, 1, None)
            sp.wait_ge(stored, 16 * (NB * B + 1))

        @block.gpsimd
        def _(pool):
            nc.gpsimd.memset(power[:], -0.5).then_inc(power_made, 1)
            pool.wait_ge(power_made, 1)
            with pool.Fori(0, NB * B) as n:
                pool.wait_ge(a_high, n + 1)
                nc.gpsimd.tensor_tensor(a_half[1][:], a_in[:], a_half[0][:].bitcast(F32), ALU.subtract).then_inc(a_low, 1)
                pool.wait_ge(variance_made, n + 1)
                nc.gpsimd.tensor_tensor(rstd[:], variance[:], power[:], ALU.pow).then_inc(rstd_made, 1)

        @block.tensor
        def _(pe):
            def attention_out(n, before):
                pe.wait_ge(a_low, n + 1)
                for tt in range(TT):
                    pe.wait_ge(v_free, n * (2 * TT) + (before + tt + 1))
                    products(nc, v_bank[tt][:], lambda s, c: a_half[s][:, c, tt * P:(tt + 1) * P],
                             lambda s, c: wo[s][:, c, :]).then_inc(o_done, 1)

            def turn(n):
                pe.wait_ge(normalised, n + 1)
                for c in range(C):
                    pe.wait_ge(t_free, n * C + (c + 1))
                    for tt in range(TT):
                        last = nc.tensor.transpose(t_bank[c % 2][:, tt * P:(tt + 1) * P], xn[:, tt, c * P:(c + 1) * P], ident[:])
                    last.then_inc(turned, 1)

            def stage(n, ahead):
                pe.wait_ge(mix_low, n * (2 * C) + C)
                for o in range(C):
                    pe.wait_ge(a_free, n * (C + TT) + (o + 1))
                    products(nc, a_bank[o % 2][:], lambda s, c: wk[s][:, c, o * P:(o + 1) * P],
                             lambda s, c: xk[s][:, c, :]).then_inc(k_done, 1)
                if ahead:
                    attention_out(n + 1, -TT)
                pe.wait_ge(mix_low, n * (2 * C) + 2 * C)
                for tt in range(TT):
                    pe.wait_ge(a_free, n * (C + TT) + (C + tt + 1))
                    products(nc, a_bank[tt % 2][:], lambda s, c: xr[s][:, c, tt * P:(tt + 1) * P],
                             lambda s, c: wr[s][:, c, :]).then_inc(r_done, 1)
                if ahead:
                    turn(n + 1)
                pe.wait_ge(kact_low, n * C + 2 * C)
                for tt in range(TT):
                    pe.wait_ge(v_free, n * (2 * TT) + ((2 if ahead else 1) * TT + tt + 1))
                    products(nc, v_bank[tt][:], lambda s, c: kact[s][:, c, tt * P:(tt + 1) * P],
                             lambda s, c: wv[s][:, c, :]).then_inc(v_done, 1)

            attention_out(0, 0)
            turn(0)
            with pe.Fori(0, NB * B - 1) as n:
                stage(n, True)
            stage(NB * B - 1, False)

        @block.scalar
        def _(act):
            def a_split(n, first=False):
                act.wait_ge(a_loaded, n * 16 + 16)
                if not first:
                    act.wait_ge(o_done, n * TT)
                nc.scalar.activation(a_half[0][:], a_in[:], ACT.Copy).then_inc(a_high, 1)

            def turned_copy(n):
                act.wait_ge(carried, n + 1)
                for c in range(C):
                    act.wait_ge(turned, n * C + (c + 1))
                    nc.scalar.activation(xT[:, c, 1:1 + BLK], t_bank[c % 2][:], ACT.Copy).then_inc(t_free, 1)

            def mix_split(n, k):
                for c in range(C):
                    act.wait_ge(mix_made, n * (2 * C) + (k * C + c + 1))
                    nc.scalar.activation((xk, xr)[k][0][:, c, :], mixed[c][:], ACT.Copy).then_inc(mix_high, 1)

            def square_high(n, o):
                act.wait_ge(square_made, n * C + (o + 1))
                nc.scalar.activation(kact[0][:, o, :], act_sq[o][:], ACT.Copy).then_inc(kact_high, 1)

            def stage(n, ahead):
                if ahead:
                    a_split(n + 1)
                for o in range(C):
                    act.wait_ge(k_done, n * C + (o + 1))
                    act.wait_ge(kact_low, n * C + (o + 1))
                    nc.scalar.activation(act_sq[o][:], a_bank[o % 2][:], ACT.Relu).then_inc(a_free, 1)
                    if o:
                        square_high(n, o - 1)
                square_high(n, C - 1)
                act.wait_ge(final_made, n * TT + TT)
                for tt in range(TT):
                    act.wait_ge(r_done, n * TT + (tt + 1))
                    nc.scalar.activation(gate[:, tt, :], a_bank[tt % 2][:], ACT.Sigmoid).then_inc(a_free, 1)
                if ahead:
                    turned_copy(n + 1)
                    mix_split(n + 1, 0)
                    mix_split(n + 1, 1)

            a_split(0, first=True)
            turned_copy(0)
            mix_split(0, 0)
            mix_split(0, 1)
            with act.Fori(0, NB * B - 1) as n:
                stage(n, True)
            stage(NB * B - 1, False)

        @block.vector
        def _(dve):
            dve.sem_inc(t_free, 2)
            dve.sem_inc(a_free, 2)
            dve.sem_inc(v_free, TT)
            dve.sem_inc(kact_low, C)
            dve.sem_inc(final_made, TT)
            dve.sem_inc(stored, 16)
            dve.wait_ge(mu_loaded, 32)
            for k in range(2):
                nc.vector.tensor_scalar(rest[k][:], mus[k][:], -1.0, 1.0, ALU.mult, ALU.add).then_inc(rest_made, 1)
            nc.vector.memset(xT[:, :, 0:1], 0.0).then_inc(carried, 1)
            dve.wait_ge(rest_made, 2)

            def residual(i, j, before):
                n = NB * i + j
                dve.wait_ge(x_loaded[j], i * 16 + 16)
                for tt in range(TT):
                    dve.wait_ge(o_done, n * TT + (tt + 1))
                    nc.vector.tensor_tensor(x1[j][:, tt, :], v_bank[tt][:], x1[j][:, tt, :], ALU.add).then_inc(v_free, 1)
                for tt in range(TT):
                    dve.wait_ge(v_free, n * (2 * TT) + (TT + before + tt + 1))
                    last = nc.vector.bn_stats(stats[:, tt, :], x1[j][:, tt, :])
                last.then_inc(stats_made, 1)
                dve.wait_ge(stats_made, n + 1)
                dve.sem_inc(stats_seen, 1)
                for tt in range(TT):
                    last = nc.vector.bn_aggr(moments[:, tt, :], stats[:, tt, :])
                last.then_inc(moments_made, 1)
                dve.wait_ge(moments_made, n + 1)
                nc.vector.tensor_scalar(variance[:], moments[:, :, 1], EPS, None, ALU.add).then_inc(variance_made, 1)
                dve.wait_ge(rstd_made, n + 1)
                for tt in range(TT):
                    last = nc.vector.tensor_scalar(xn[:, tt, :], x1[j][:, tt, :], moments[:, tt, 0:1],
                                                   rstd[:, tt:tt + 1], ALU.subtract, ALU.mult)
                last.then_inc(normalised, 1)

            def mix(n, k):
                m = n * (2 * C) + k * C

                def part_of(c):
                    dve.wait_ge(t_free, n * C + (2 + c + 1))
                    if c == 3:
                        dve.wait_ge(mix_made, m + 1)
                    nc.vector.tensor_scalar(part[c % 3][:], xT[:, c, 0:BLK], rest[1 - k][:, c:c + 1], None, ALU.mult
                                            ).then_inc(part_made, 1)

                def whole(c):
                    dve.wait_ge(part_made, m + (c + 1))
                    nc.vector.scalar_tensor_tensor(mixed[c][:], xT[:, c, 1:1 + BLK], mus[1 - k][:, c:c + 1], part[c % 3][:],
                                                   ALU.mult, ALU.add).then_inc(mix_made, 1)

                def low(c):
                    dve.wait_ge(mix_high, m + (c + 1))
                    nc.vector.tensor_tensor((xk, xr)[k][1][:, c, :], mixed[c][:], (xk, xr)[k][0][:, c, :].bitcast(F32),
                                            ALU.subtract).then_inc(mix_low, 1)

                part_of(0)
                for c in range(C):
                    if c + 1 < C:
                        part_of(c + 1)
                    whole(c)
                    if c:
                        low(c - 1)
                low(C - 1)

            def carry(j):
                if j == NB - 1:
                    nc.vector.memset(xT[:, :, 0:1], 0.0).then_inc(carried, 1)
                else:
                    nc.vector.tensor_copy(xT[:, :, 0:1], xT[:, :, BLK:BLK + 1]).then_inc(carried, 1)

            def stage(i, j, ahead):
                n = NB * i + j

                def square(o):
                    dve.wait_ge(a_free, n * (C + TT) + (2 + o + 1))
                    nc.vector.tensor_tensor(act_sq[o][:], act_sq[o][:], act_sq[o][:], ALU.mult).then_inc(square_made, 1)

                def square_low(o):
                    dve.wait_ge(kact_high, n * C + (o + 1))
                    nc.vector.tensor_tensor(kact[1][:, o, :], act_sq[o][:], kact[0][:, o, :].bitcast(F32), ALU.subtract
                                            ).then_inc(kact_low, 1)

                square(0)
                for o in range(1, C):
                    square(o)
                    square_low(o - 1)
                square_low(C - 1)
                if ahead:
                    i1, j1 = ahead
                    residual(i1, j1, -TT)
                    mix(NB * i1 + j1, 0)
                    mix(NB * i1 + j1, 1)
                    carry(j1)
                dve.wait_ge(stored, n * 16 + 16)
                dve.wait_ge(a_free, n * (C + TT) + (2 + C + TT))
                for tt in range(TT):
                    dve.wait_ge(v_done, n * TT + (tt + 1))
                    nc.vector.tensor_tensor(final[:, tt, :], v_bank[tt][:], gate[:, tt, :], ALU.mult).then_inc(v_free, 1)
                for tt in range(TT):
                    dve.wait_ge(v_free, n * (2 * TT) + (TT + (2 if ahead else 1) * TT + tt + 1))
                    nc.vector.tensor_tensor(final[:, tt, :], final[:, tt, :], x1[j][:, tt, :], ALU.add).then_inc(final_made, 1)

            residual(0, 0, 0)
            mix(0, 0)
            mix(0, 1)
            carry(0)
            with dve.Fori(0, B - 1) as i:
                stage(i, 0, (i, 1))
                stage(i, 1, (i + 1, 0))
            stage(B - 1, 0, (B - 1, 1))
            stage(B - 1, 1, None)


def block_program(nc, x, context, mask, wq, wk, wv, wo, wr, wkf, wvf, mu_r, mu_k, out):
    q_half = [nc.dram_tensor(f"q_half{s}", (B, G, P, L), F32) for s in range(2)]
    k_half = [nc.dram_tensor(f"k_half{s}", (B, G, P, L), F32) for s in range(2)]
    v_rows = nc.dram_tensor("v_rows", (B, G, P, KC, P), F32)
    mask_rows = nc.dram_tensor("mask_rows", (NG, L), F32)
    attended = nc.dram_tensor("attended", (NG, P, L), F32)
    with ExitStack() as ctx:
        ident = ctx.enter_context(nc.sbuf_tensor("ident", [P, P], F32))
        identity_made = ctx.enter_context(nc.semaphore("identity_made"))
        w = [[ctx.enter_context(nc.sbuf_tensor(f"w{k}_{s}", [P, C, D], F32R)) for s in range(2)] for k in range(4)]
        prepare_weights(nc, "qkv", [wq, wk, wv], w[:3], ident, identity_made, True, mask, mask_rows.ap())
        project(nc, x, context, w[0], w[1], w[2], ident,
                [t.ap().rearrange("b g p t -> b p g t") for t in q_half],
                [t.ap().rearrange("b g p t -> b p g t") for t in k_half], v_rows.ap())

        attend(nc, [t.ap().rearrange("b g p t -> (b g) p t") for t in q_half],
               [t.ap().rearrange("b g p t -> (b g) p t") for t in k_half],
               v_rows.ap().rearrange("b g p c d -> (b g) p c d"), mask_rows.ap(), ident, attended.ap())

        prepare_weights(nc, "ork", [wo, wr, wkf, wvf], w, ident, identity_made, False)
        finish(nc, x, attended.ap().rearrange("(b g) p t -> b g p t", g=G), (mu_r, mu_k), w[0], w[1], w[2], w[3], ident, out)


_INS = ['x', 'ctx_1024', 'mask_Bx1x1xS2_bf1', 'L0_xattn_Wq', 'L0_xattn_Wk', 'L0_xattn_Wv', 'L0_xattn_Wo',
        'L0_ffn_W_r', 'L0_ffn_W_k', 'L0_ffn_W_v', 'L0_ffn_mu_r', 'L0_ffn_mu_k']


def kernel(**inputs):
    import numpy as _np
    import concourse.bacc as _bacc
    from concourse import mybir as _mybir
    from concourse.bass_utils import run_bass_kernel_spmd as _run

    nc = _bacc.Bacc("TRN2", target_bir_lowering=False, num_devices=1)
    arrays, args = {}, []
    for name in _INS:
        a = _np.ascontiguousarray(inputs[name])
        arrays[f"in_{name}_dram"] = a
        args.append(nc.dram_tensor(f"in_{name}_dram", a.shape, _mybir.dt.from_np(a.dtype), kind="ExternalInput").ap())
    args.append(nc.dram_tensor("out_0_dram", (8, 1024, 512), _mybir.dt.float32, kind="ExternalOutput").ap())
    block_program(nc, *args)
    r = _run(nc, [arrays], core_ids=[0])
    return r.results[0]["out_0_dram"]
```

```python
from contextlib import ExitStack

import concourse.bass as bass
from concourse import mybir
from concourse.alu_op_type import AluOpType as ALU

F32 = mybir.dt.float32
F32R = mybir.dt.float32r
U8 = mybir.dt.uint8
ACT = mybir.ActivationFunctionType

B, L, D = 8, 1024, 512
H, DH = 16, 32
P = 128
C = D // P
BLK = 512
NB = L // BLK
TT = BLK // P
HG = P // DH
G = H // HG
QT = L // P
KC = L // P
NG = B * G
STACK = 3 * DH + 1
EPS = 1e-5
SCALE = float(1.0 / DH ** 0.5)
MASKED = float(2.0 ** 120)


def products(nc, out, stat, mov):
    n = 0
    for c in range(C):
        for s, m in ((1, 0), (0, 1), (0, 0)):
            last = nc.tensor.matmul(out, stat(s, c), mov(m, c), start=n == 0, stop=n == 3 * C - 1)
            n += 1
    return last


def make_identity(nc, ident, made):
    nc.gpsimd.memset(ident[:], 0.0).then_inc(made, 1)
    nc.gpsimd.wait_ge(made, 1)
    nc.gpsimd.affine_select(out=ident[:], in_=ident[:], compare_op=ALU.not_equal, fill=1.0, base=0,
                            pattern=[[-1, P]], channel_multiplier=1).then_inc(made, 1)


def prepare_weights(nc, tag, weights, halves, ident, identity_made, first, mask=None, mask_rows=None):
    with ExitStack() as ctx:
        nat = [ctx.enter_context(nc.sbuf_tensor(f"{tag}_nat{k}", [P, C, D], F32)) for k in range(len(weights))]
        banks = [ctx.enter_context(nc.psum_tensor(f"{tag}_bank{k}", [P, D], F32)) for k in range(4)]
        loaded = [ctx.enter_context(nc.semaphore(f"{tag}_loaded{k}")) for k in range(len(weights))]
        transposed = ctx.enter_context(nc.semaphore(f"{tag}_transposed"))
        high_made = ctx.enter_context(nc.semaphore(f"{tag}_high"))
        low_made = ctx.enter_context(nc.semaphore(f"{tag}_low"))
        if mask is not None:
            mask_in = ctx.enter_context(nc.sbuf_tensor("mask_in", [B, L], U8))
            mask_row = ctx.enter_context(nc.sbuf_tensor("mask_row", [B, L], F32R))
            mask_loaded = ctx.enter_context(nc.semaphore("mask_loaded"))
            mask_made = ctx.enter_context(nc.semaphore("mask_made"))
            mask_stored = ctx.enter_context(nc.semaphore("mask_stored"))
        block = ctx.enter_context(nc.Block())

        @block.sync
        def _(sp):
            for k, w in enumerate(weights):
                sp.dma_start(nat[k][:], w.rearrange("(o p) c -> p o c", p=P)).then_inc(loaded[k], 16)
            if mask is not None:
                sp.dma_start(mask_in[:], mask.rearrange("b x y k -> (b x y) k")).then_inc(mask_loaded, 16)
                sp.wait_ge(mask_made, 1)
                for g in range(G):
                    sp.dma_start(mask_rows.rearrange("(b g) k -> g b k", g=G)[g],
                                 mask_row[:].bitcast(F32)).then_inc(mask_stored, 16)
                sp.wait_ge(mask_stored, 16 * G)

        @block.gpsimd
        def _(pool):
            if first:
                make_identity(nc, ident, identity_made)

        @block.tensor
        def _(pe):
            pe.wait_ge(identity_made, 2)
            for k in range(len(weights)):
                pe.wait_ge(loaded[k], 16)
                for c in range(C):
                    n = k * C + c
                    if n >= 4:
                        pe.wait_ge(low_made, n - 3)
                    for o in range(C):
                        last = nc.tensor.transpose(banks[n % 4][:, o * P:(o + 1) * P],
                                                   nat[k][:, o, c * P:(c + 1) * P], ident[:])
                    last.then_inc(transposed, 1)

        @block.scalar
        def _(act):
            for k in range(len(weights)):
                for c in range(C):
                    n = k * C + c
                    act.wait_ge(transposed, n + 1)
                    nc.scalar.activation(halves[k][0][:, c, :], banks[n % 4][:], ACT.Copy).then_inc(high_made, 1)

        @block.vector
        def _(dve):
            for k in range(len(weights)):
                for c in range(C):
                    n = k * C + c
                    dve.wait_ge(high_made, n + 1)
                    nc.vector.tensor_tensor(halves[k][1][:, c, :], banks[n % 4][:],
                                            halves[k][0][:, c, :].bitcast(F32), ALU.subtract).then_inc(low_made, 1)
            if mask is not None:
                dve.wait_ge(mask_loaded, 16)
                nc.vector.tensor_scalar(mask_row[:], mask_in[:], MASKED, -MASKED, ALU.mult, ALU.add).then_inc(mask_made, 1)


def project(nc, x, ctx_in, wq, wk, wv, ident, q_half, k_half, v_rows, q_scale=SCALE):
    with ExitStack() as ctx:
        def sb(name, shape, dt=F32):
            return ctx.enter_context(nc.sbuf_tensor("a_" + name, shape, dt))

        def sem(name):
            return ctx.enter_context(nc.semaphore("a_" + name))

        x_in = [sb(f"x_in{j}", [P, TT, D]) for j in range(NB)]
        c_in = [sb(f"c_in{j}", [P, TT, D]) for j in range(NB)]
        xT = [sb(f"xT{s}", [P, C, BLK], F32R) for s in range(2)]
        cT = [sb(f"cT{s}", [P, C, BLK], F32R) for s in range(2)]
        q_out = [sb(f"q_out{s}", [P, C, BLK], F32R) for s in range(2)]
        k_out = [sb(f"k_out{s}", [P, C, BLK], F32R) for s in range(2)]
        v_out = sb("v_out", [P, TT, D])
        stats = sb("stats", [P, TT, 6])
        moments = sb("moments", [P, TT, 2])
        power = sb("power", [P, TT])
        variance = sb("variance", [P, TT])
        rstd = sb("rstd", [P, TT])
        t_bank = [ctx.enter_context(nc.psum_tensor(f"a_t{k}", [P, BLK], F32)) for k in range(2)]
        p_bank = [ctx.enter_context(nc.psum_tensor(f"a_p{k}", [P, BLK], F32)) for k in range(6)]
        x_loaded = [sem(f"x_loaded{j}") for j in range(NB)]
        c_loaded = [sem(f"c_loaded{j}") for j in range(NB)]
        PB = 3 * C
        power_made = sem("power_made")
        stats_made = sem("stats_made")
        stats_seen = sem("stats_seen")
        moments_made = sem("moments_made")
        variance_made = sem("variance_made")
        rstd_made = sem("rstd_made")
        normalised = sem("normalised")
        x_turned = sem("x_turned")
        c_turned = sem("c_turned")
        turned_high = sem("turned_high")
        t_free = sem("t_free")
        projected = sem("projected")
        out_high = sem("out_high")
        bank_free = sem("bank_free")
        q_stored = sem("q_stored")
        k_stored = sem("k_stored")
        v_stored = sem("v_stored")
        block = ctx.enter_context(nc.Block())

        @block.sync
        def _(sp):
            def load_x(i, j):
                sp.dma_start(x_in[j][:], x[i, j * BLK:(j + 1) * BLK, :].rearrange("(t p) c -> p t c", p=P)
                             ).then_inc(x_loaded[j], 16)

            def load_c(i, j):
                sp.dma_start(c_in[j][:], ctx_in[i, j * BLK:(j + 1) * BLK, :].rearrange("(t p) c -> p t c", p=P)
                             ).then_inc(c_loaded[j], 16)

            def store(i, j):
                n = NB * i + j
                for first, out, half, stored in ((0, q_out, q_half, q_stored), (C, k_out, k_half, k_stored)):
                    sp.wait_ge(bank_free, n * PB + (6 + first + C))
                    for s in range(2):
                        sp.dma_start(half[s][i, :, :, j * BLK:(j + 1) * BLK], out[s][:].bitcast(F32)
                                     ).then_inc(stored, 16)
                sp.wait_ge(bank_free, n * PB + (6 + PB))
                for g in range(G):
                    sp.dma_start(v_rows[i, g, :, j * TT:(j + 1) * TT, :], v_out[:, :, g * P:(g + 1) * P]
                                 ).then_inc(v_stored, 16)

            for j in range(NB):
                load_x(0, j)
                load_c(0, j)
            with sp.Fori(0, B - 1) as i:
                for j in range(NB):
                    sp.wait_ge(c_turned, (NB * i + j) * C + C)
                    load_c(i + 1, j)
                    sp.wait_ge(x_turned, (NB * i + j) * C + C)
                    load_x(i + 1, j)
                    store(i, j)
            for j in range(NB):
                store(B - 1, j)
            sp.wait_ge(q_stored, 32 * (NB * B + 1))
            sp.wait_ge(k_stored, 32 * (NB * B + 1))
            sp.wait_ge(v_stored, 16 * G * (NB * B + 1))

        @block.tensor
        def _(pe):
            def turn(src, i, j, before, turned):
                for c in range(C):
                    pe.wait_ge(t_free, (NB * i + j) * 2 * C + (before + c + 1))
                    for tt in range(TT):
                        last = nc.tensor.transpose(t_bank[c % 2][:, tt * P:(tt + 1) * P],
                                                   src[:, tt, c * P:(c + 1) * P], ident[:])
                    last.then_inc(turned, 1)

            def turn_x(i, j):
                pe.wait_ge(normalised, (NB * i + j) + 1)
                turn(x_in[j], i, j, 0, x_turned)

            def turn_c(i, j):
                pe.wait_ge(c_loaded[j], i * 16 + 16)
                turn(c_in[j], i, j, C, c_turned)

            def stage(i, j, ahead):
                n = NB * i + j
                turn_c(i, j)
                for first, w, src in ((0, wq, xT), (C, wk, cT)):
                    pe.wait_ge(t_free, n * 2 * C + (2 + C + first))
                    for o in range(C):
                        pe.wait_ge(bank_free, n * PB + (first + o + 1))
                        products(nc, p_bank[(first + o) % 6][:], lambda s, c: w[s][:, c, o * P:(o + 1) * P],
                                 lambda s, c: src[s][:, c, :]).then_inc(projected, 1)
                if ahead:
                    turn_x(*ahead)
                for tt in range(TT):
                    pe.wait_ge(bank_free, n * PB + (2 * C + tt + 1))
                    products(nc, p_bank[(2 * C + tt) % 6][:], lambda s, c: cT[s][:, c, tt * P:(tt + 1) * P],
                             lambda s, c: wv[s][:, c, :]).then_inc(projected, 1)

            turn_x(0, 0)
            with pe.Fori(0, B - 1) as i:
                stage(i, 0, (i, 1))
                stage(i, 1, (i + 1, 0))
            stage(B - 1, 0, (B - 1, 1))
            stage(B - 1, 1, None)

        @block.gpsimd
        def _(pool):
            nc.gpsimd.memset(power[:], -0.5).then_inc(power_made, 1)
            pool.wait_ge(power_made, 1)
            with pool.Fori(0, NB * B) as n:
                pool.wait_ge(variance_made, n + 1)
                nc.gpsimd.tensor_tensor(rstd[:], variance[:], power[:], ALU.pow).then_inc(rstd_made, 1)

        @block.scalar
        def _(act):
            act.sem_inc(q_stored, 32)
            act.sem_inc(k_stored, 32)

            def split_high(i, j, dst, turned):
                for c in range(C):
                    act.wait_ge(turned, (NB * i + j) * C + (c + 1))
                    nc.scalar.activation(dst[:, c, :], t_bank[c % 2][:], ACT.Copy).then_inc(turned_high, 1)

            def stage(i, j, ahead):
                n = NB * i + j
                split_high(i, j, cT[0], c_turned)
                for out, stored, first, scale in ((q_out, q_stored, 0, SCALE), (k_out, k_stored, C, 1.0)):
                    act.wait_ge(stored, n * 32 + 32)
                    for o in range(C):
                        act.wait_ge(projected, n * PB + (first + o + 1))
                        nc.scalar.activation(out[0][:, o, :], p_bank[(first + o) % 6][:], ACT.Copy, scale=scale
                                             ).then_inc(out_high, 1)
                if ahead:
                    split_high(*ahead, xT[0], x_turned)

            split_high(0, 0, xT[0], x_turned)
            with act.Fori(0, B - 1) as i:
                stage(i, 0, (i, 1))
                stage(i, 1, (i + 1, 0))
            stage(B - 1, 0, (B - 1, 1))
            stage(B - 1, 1, None)

        @block.vector
        def _(dve):
            dve.sem_inc(t_free, 2)
            dve.sem_inc(bank_free, 6)
            dve.sem_inc(v_stored, 16 * G)

            def moments_of(i, j):
                n = NB * i + j
                dve.wait_ge(x_loaded[j], i * 16 + 16)
                for tt in range(TT):
                    last = nc.vector.bn_stats(stats[:, tt, :], x_in[j][:, tt, :])
                last.then_inc(stats_made, 1)
                dve.wait_ge(stats_made, n + 1)
                dve.sem_inc(stats_seen, 1)
                for tt in range(TT):
                    last = nc.vector.bn_aggr(moments[:, tt, :], stats[:, tt, :])
                last.then_inc(moments_made, 1)
                dve.wait_ge(moments_made, n + 1)
                nc.vector.tensor_scalar(variance[:], moments[:, :, 1], EPS, None, ALU.add).then_inc(variance_made, 1)

            def normalise(i, j):
                dve.wait_ge(rstd_made, (NB * i + j) + 1)
                for tt in range(TT):
                    last = nc.vector.tensor_scalar(x_in[j][:, tt, :], x_in[j][:, tt, :], moments[:, tt, 0:1],
                                                   rstd[:, tt:tt + 1], ALU.subtract, ALU.mult)
                last.then_inc(normalised, 1)

            def split_low(i, j, before, dst):
                for c in range(C):
                    dve.wait_ge(turned_high, (NB * i + j) * 2 * C + (before + c + 1))
                    nc.vector.tensor_tensor(dst[1][:, c, :], t_bank[c % 2][:], dst[0][:, c, :].bitcast(F32),
                                            ALU.subtract).then_inc(t_free, 1)

            def stage(i, j, ahead):
                n = NB * i + j
                split_low(i, j, C, cT)
                if ahead:
                    moments_of(*ahead)
                for out, first, scale in ((q_out, 0, SCALE), (k_out, C, 1.0)):
                    for o in range(C):
                        dve.wait_ge(out_high, n * 2 * C + (first + o + 1))
                        nc.vector.scalar_tensor_tensor(out[1][:, o, :], p_bank[(first + o) % 6][:], scale,
                                                       out[0][:, o, :].bitcast(F32), ALU.mult, ALU.subtract
                                                       ).then_inc(bank_free, 1)
                    if ahead and first == 0:
                        normalise(*ahead)
                if ahead:
                    split_low(*ahead, 0, xT)
                dve.wait_ge(v_stored, n * (16 * G) + 16 * G)
                for tt in range(TT):
                    dve.wait_ge(projected, n * PB + (2 * C + tt + 1))
                    nc.vector.tensor_copy(v_out[:, tt, :], p_bank[(2 * C + tt) % 6][:]).then_inc(bank_free, 1)

            moments_of(0, 0)
            normalise(0, 0)
            split_low(0, 0, 0, xT)
            with dve.Fori(0, B - 1) as i:
                stage(i, 0, (i, 1))
                stage(i, 1, (i + 1, 0))
            stage(B - 1, 0, (B - 1, 1))
            stage(B - 1, 1, None)

def attend(nc, q_half, k_half, v_rows, mask_rows, inverse_rows, ident, attended):
    with ExitStack() as ctx:
        def sb(name, shape, dt=F32):
            return ctx.enter_context(nc.sbuf_tensor("b_" + name, shape, dt))

        def sem(name):
            return ctx.enter_context(nc.semaphore("b_" + name))

        U = KC * HG
        HALVES = 2 * HG * QT
        M0, M1, TURN = 3, 28, 28
        SUMS, INVERT, DIVIDE = 4, 12, TURN
        RING = 4
        ADDED = 6
        A = HG * (ADDED - 1)
        W = HG * L // P
        q_stack = [sb(f"q_stack{p}", [STACK + 2, HG, L], F32R) for p in range(2)]
        k_stack = [sb(f"k_stack{p}", [STACK + 2, HG, L], F32R) for p in range(2)]
        v_in = [sb(f"v_in{p}", [P, KC, P]) for p in range(2)]
        prob = [sb(f"prob{k}", [P, HG, L]) for k in range(RING)]
        acc = [sb(f"acc{p}", [P, HG, L]) for p in range(2)]
        neg_max = sb("neg_max", [P, HG * QT, 2])
        neg_row_max = sb("neg_row_max", [P, HG * QT])
        max_half = [sb(f"max_half{s}", [HG * QT, P], F32R) for s in range(2)]
        ones_block = sb("ones_block", [P, DH])
        sums = sb("sums", [P, L])
        sums_in = sb("sums_in", [P, W])
        inverse = sb("inverse", [P, W])
        inverse_wide = sb("inverse_wide", [P, L])
        raw = sb("raw", [P, L])
        result = [sb(f"result{p}", [P, L]) for p in range(2)]
        m_bank = [ctx.enter_context(nc.psum_tensor(f"b_m{k}", [P, BLK], F32)) for k in range(2)]
        score = [ctx.enter_context(nc.psum_tensor(f"b_score{k}", [P, L], F32)) for k in range(2)]
        out_bank = ctx.enter_context(nc.psum_tensor("b_out", [P, L], F32))
        ones_made = sem("ones_made")
        ones_set = sem("ones_set")
        block_made = sem("block_made")
        head_loaded = [[sem(f"head_loaded{p}_{h}") for h in range(HG)] for p in range(2)]
        v_loaded = [sem(f"v_loaded{p}") for p in range(2)]
        m_filled = sem("m_filled")
        m_free = sem("m_free")
        row_max_made = sem("row_max_made")
        max_high = sem("max_high")
        max_set = sem("max_set")
        scored = sem("scored")
        exp_made = sem("exp_made")
        gathered = sem("gathered")
        pool_added = sem("pool_added")
        sums_moved = sem("sums_moved")
        inverse_made = sem("inverse_made")
        inverse_stored = sem("inverse_stored")
        inverse_loaded = sem("inverse_loaded")
        divided = sem("divided")
        raw_made = sem("raw_made")
        stored = [sem(f"stored{p}") for p in range(2)]
        block = ctx.enter_context(nc.Block())

        def uses(first, last):
            found = []
            for u in range(U):
                if not last and M0 <= u < M1:
                    found += [(u, "half", n) for n in range(HALVES * (u - M0) // (M1 - M0), HALVES * (u - M0 + 1) // (M1 - M0))]
                if not first and u in (SUMS, SUMS + 1):
                    found.append((u, "sums", u - SUMS))
                if not last and u == TURN:
                    found.append((u, "turn", 0))
            return found

        START = [(0, "half", n) for n in range(HALVES)] + [(0, "turn", 0)]
        FIRST, MIDDLE, LAST, END = uses(True, False), uses(False, False), uses(False, True), [
            (0, "sums", 0), (0, "sums", 1)]

        def used(g, plan):
            if plan is START:
                return 0
            if plan is FIRST:
                return len(START)
            before = len(START) + len(FIRST) - len(MIDDLE)
            return g * len(MIDDLE) + (before + (len(LAST) - len(MIDDLE) if plan is END else 0))

        def slot(p, plan, n):
            g = 2 - p if plan is MIDDLE else NG - 1 if plan is LAST else NG if plan is END else 0
            return (used(g, plan) + n) % 2

        def read(g, plan, kind):
            return used(g, plan) + (2 + max(n for n, use in enumerate(plan) if use[1] == kind) + 1)

        def filled(g, plan, kind):
            return read(g, plan, kind) - 2

        def groups(eng, group):
            group(0, 0, FIRST)
            with eng.Fori(0, NG // 2 - 1) as i:
                group(i * 2 + 1, 1, MIDDLE)
                group(i * 2 + 2, 0, MIDDLE)
            group(NG - 1, 1, LAST)

        LOADS = 7

        @block.sync
        def _(sp):
            def load_head(g, p, h):
                done = head_loaded[p][h]
                for stack, half, order in ((q_stack, q_half, (0, 0, 1)), (k_stack, k_half, (0, 1, 0))):
                    for r, s in enumerate(order):
                        sp.dma_start(stack[p][r * DH:(r + 1) * DH, h, :].bitcast(F32), half[s][g, h * DH:(h + 1) * DH, :]
                                     ).then_inc(done, 16)
                sp.dma_start(k_stack[p][STACK - 1:STACK, h, :].bitcast(F32), mask_rows[g].rearrange("(a k) -> a k", a=1)
                             ).then_inc(done, 16)

            def load_v(g, p):
                sp.dma_start(v_in[p][:], v_rows[g]).then_inc(v_loaded[p], 16)

            def set_maxima(g, p, plan):
                sp.wait_ge(m_free, read(g if plan is START else g - 1, plan, "turn"))
                for s in range(2):
                    sp.dma_start(q_stack[p][STACK + s:STACK + s + 1, :, :].bitcast(F32), max_half[s][:].bitcast(F32)
                                 ).then_inc(max_set, 16)

            def spread_inverse(g, plan):
                sp.wait_ge(m_free, read(g + 1, plan, "sums"))
                for h in range(HG):
                    sp.dma_start(sums_in[h * DH:(h + 1) * DH, :], sums[h * DH:h * DH + 1, :]).then_inc(sums_moved, 16)
                sp.wait_ge(inverse_made, g + 1)
                sp.dma_start(inverse_rows[g].rearrange("h (a w) -> (h a) w", w=W), inverse[:]).then_inc(inverse_stored, 16)
                sp.wait_ge(inverse_stored, g * 16 + 16)
                sp.wait_ge(divided, g + 1)
                for h in range(HG):
                    sp.dma_start(inverse_wide[h * DH:(h + 1) * DH, :],
                                 inverse_rows[g, h:h + 1, :].broadcast_to([DH, L])).then_inc(inverse_loaded, 16)

            def store(g, p):
                sp.wait_ge(divided, g + 2)
                sp.dma_start(attended[g], result[p][:]).then_inc(stored[p], 16)

            def group(g, p, plan):
                if plan is not FIRST:
                    if plan is MIDDLE:
                        sp.wait_ge(scored, g * U)
                        for h in range(HG):
                            load_head(g + 1, 1 - p, h)
                        sp.wait_ge(gathered, g * (2 * KC) + 2 * RING)
                        load_v(g + 1, 1 - p)
                    spread_inverse(g - 1, plan)
                if plan is not LAST:
                    set_maxima(g + 1, 1 - p, plan)
                if plan is not FIRST:
                    store(g - 1, 1 - p)

            sp.wait_ge(ones_made, 1)
            for p in range(2):
                for stack, first, rows in ((q_stack, STACK - 1, 1), (k_stack, STACK, 2)):
                    sp.dma_start(stack[p][first:first + rows, :, :].bitcast(F32),
                                 prob[0][0:rows, :, :]).then_inc(ones_set, 16)
            for p in range(2):
                for h in range(HG):
                    load_head(p, p, h)
                load_v(p, p)
            set_maxima(0, 0, START)
            groups(sp, group)
            spread_inverse(NG - 1, END)
            store(NG - 1, 1)
            for p in range(2):
                sp.wait_ge(stored[p], 16 * (NG // 2 + 1))

        @block.tensor
        def _(pe):
            def unit(g, p, u):
                if u == 0:
                    pe.wait_ge(max_set, g * 32 + 32)
                h, kc = u % HG, u // HG
                for half in range(2):
                    last = nc.tensor.matmul(score[u % 2][:, half * BLK:(half + 1) * BLK], k_stack[p][:, h, kc * P:(kc + 1) * P],
                                            q_stack[p][:, h, half * BLK:(half + 1) * BLK], start=True, stop=True)
                last.then_inc(scored, 1)

            def gather(g, p, kc, half):
                if kc == 0 and half == 0:
                    pe.wait_ge(raw_made, g + 1)
                    pe.wait_ge(v_loaded[p], (g - p) * 8 + 16)
                pe.wait_ge(exp_made, g * U + (kc * HG + HG))
                for h in range(HG):
                    last = nc.tensor.matmul(out_bank[h * DH:(h + 1) * DH, half * BLK:(half + 1) * BLK],
                                            v_in[p][:, kc, h * DH:(h + 1) * DH], prob[kc % RING][:, h, half * BLK:(half + 1) * BLK],
                                            start=kc == 0, stop=kc == KC - 1, tile_position=(0, h * DH))
                last.then_inc(gathered, 1)

            def m_use(g, p, plan, n):
                _, kind, k = plan[n]
                bank = m_bank[slot(p, plan, n)]
                pe.wait_ge(m_free, used(g, plan) + (n + 1))
                if kind == "half":
                    after, q = (g, p) if plan is START else (g + 1, 1 - p), k // 2
                    h, qt = q // QT, q % QT
                    if k % (2 * QT) == 0:
                        pe.wait_ge(head_loaded[after[1]][h], (after[0] - after[1]) * (8 * LOADS) + 16 * LOADS)
                    last = nc.tensor.matmul(bank[:], q_stack[after[1]][0:STACK, h, qt * P:(qt + 1) * P],
                                            k_stack[after[1]][0:STACK, h, k % 2 * BLK:(k % 2 + 1) * BLK], start=True, stop=True)
                elif kind == "turn":
                    pe.wait_ge(row_max_made, g + (1 if plan is START else 2))
                    last = nc.tensor.transpose(bank[0:HG * QT, 0:P], neg_row_max[:], ident[:])
                else:
                    pe.wait_ge(pool_added, (g + 1) * A)
                    parts = [acc[1 - p]] + [prob[kc % RING] for kc in range(ADDED, KC)]
                    for r, part in enumerate(parts):
                        for h in range(HG):
                            last = nc.tensor.matmul(bank[h * DH:(h + 1) * DH, :], ones_block[:], part[:, h, k * BLK:(k + 1) * BLK],
                                                    start=r == 0, stop=r == len(parts) - 1, tile_position=(0, h * DH))
                last.then_inc(m_filled, 1)

            def group(g, p, plan):
                for u in range(U):
                    here = [n for n, use in enumerate(plan) if use[0] == u]
                    for n in here[:1]:
                        m_use(g, p, plan, n)
                    if u + 2 < U:
                        pe.wait_ge(exp_made, g * U + (u + 1))
                        unit(g, p, u + 2)
                    elif plan is not LAST:
                        pe.wait_ge(exp_made, g * U + (u + 1))
                        unit(g + 1, 1 - p, u + 2 - U)
                    for n in here[1:]:
                        m_use(g, p, plan, n)
                    if u % 4 in (1, 3):
                        if u > 4:
                            gather(g, p, u // 4 - 1, u % 4 // 2)
                        elif plan is not FIRST:
                            gather(g - 1, 1 - p, KC - 1, u % 4 // 2)

            pe.sem_inc(gathered, 2 * RING)
            pe.wait_ge(block_made, 1)
            pe.wait_ge(ones_set, 64)
            for n in range(len(START)):
                m_use(0, 0, START, n)
            unit(0, 0, 0)
            unit(0, 0, 1)
            groups(pe, group)
            gather(NG - 1, 1, KC - 1, 0)
            gather(NG - 1, 1, KC - 1, 1)
            for n in range(len(END)):
                m_use(NG, 0, END, n)

        @block.gpsimd
        def _(pool):
            nc.gpsimd.memset(prob[0][0:2, :, :], 1.0).then_inc(ones_made, 1)
            nc.gpsimd.memset(ones_block[:], 1.0).then_inc(block_made, 1)
            pool.sem_inc(pool_added, A)

            def group(g, p, plan):
                if plan is not FIRST:
                    pool.wait_ge(m_filled, filled(g - 1, MIDDLE, "sums"))
                for kc in range(1, ADDED):
                    for h in range(HG):
                        pool.wait_ge(exp_made, g * U + (kc * HG + h + 1))
                        if kc > 1:
                            pool.wait_ge(pool_added, (g + 1) * A + (HG * (kc - 2) + h + 1))
                        nc.gpsimd.tensor_tensor(acc[p][:, h, :], prob[0][:, h, :] if kc == 1 else acc[p][:, h, :],
                                                prob[kc % RING][:, h, :], ALU.add).then_inc(pool_added, 1)

            groups(pool, group)

        @block.scalar
        def _(act):
            act.sem_inc(raw_made, 1)
            act.wait_ge(ones_set, 64)

            def maxima_high(g, p, plan):
                act.wait_ge(m_filled, read(g if plan is START else g - 1, plan, "turn") - 2)
                if plan is not START:
                    act.wait_ge(max_set, g * 32)
                nc.scalar.activation(max_half[0][:], m_bank[slot(p, plan, len(plan) - 1)][0:HG * QT, 0:P], ACT.Copy
                                     ).then_inc(max_high, 1)

            def group(g, p, plan):
                for u in range(U):
                    h, kc = u % HG, u // HG
                    act.wait_ge(scored, g * U + (u + 1))
                    if h == 0:
                        act.wait_ge(gathered, g * (2 * KC) + (2 * kc + 2))
                    if kc >= RING:
                        act.wait_ge(pool_added, (g + 1) * A + (HG * (max(kc - RING, 1) - 1) + h + 1))
                    elif kc + KC - RING < ADDED:
                        act.wait_ge(pool_added, g * A + (HG * (kc + KC - RING - 1) + h + 1))
                    elif plan is not FIRST and h == 0:
                        act.wait_ge(m_filled, filled(g, plan, "sums"))
                    nc.scalar.activation(prob[kc % RING][:, h, :], score[u % 2][:], ACT.Exp).then_inc(exp_made, 1)
                    if plan is not FIRST and u == 5:
                        act.wait_ge(divided, g)
                        act.wait_ge(gathered, g * (2 * KC) + 2 * RING)
                        nc.scalar.activation(raw[:], out_bank[:], ACT.Copy).then_inc(raw_made, 1)
                    if plan is not LAST and u == TURN + 1:
                        maxima_high(g + 1, p, plan)

            maxima_high(0, 0, START)
            groups(act, group)
            act.wait_ge(divided, NG)
            act.wait_ge(gathered, NG * (2 * KC) + 2 * RING)
            nc.scalar.activation(raw[:], out_bank[:], ACT.Copy).then_inc(raw_made, 1)

        @block.vector
        def _(dve):
            dve.sem_inc(m_free, 2)
            dve.sem_inc(divided, 1)
            dve.sem_inc(sums_moved, 16)
            for p in range(2):
                dve.sem_inc(stored[p], 16)

            def m_use(g, p, plan, n):
                _, kind, k = plan[n]
                bank = m_bank[slot(p, plan, n)]
                dve.wait_ge(m_filled, used(g, plan) + (n + 1))
                if kind == "half":
                    nc.vector.tensor_reduce(neg_max[:, k // 2, k % 2:k % 2 + 1], bank[:], mybir.AxisListType.X, ALU.max,
                                            negate=True).then_inc(m_free, 1)
                    if k == HALVES - 1:
                        dve.wait_ge(m_free, used(g, plan) + (2 + n + 1))
                        nc.vector.tensor_tensor(neg_row_max[:], neg_max[:, :, 0], neg_max[:, :, 1], ALU.min
                                                ).then_inc(row_max_made, 1)
                elif kind == "turn":
                    dve.wait_ge(max_high, g + (1 if plan is START else 2))
                    nc.vector.tensor_tensor(max_half[1][:], bank[0:HG * QT, 0:P], max_half[0][:].bitcast(F32), ALU.subtract
                                            ).then_inc(m_free, 1)
                else:
                    if k == 0:
                        dve.wait_ge(sums_moved, (g - 1) * 64 + 16)
                    nc.vector.tensor_copy(sums[:, k * BLK:(k + 1) * BLK], bank[:]).then_inc(m_free, 1)

            def invert(g):
                dve.wait_ge(sums_moved, g * 64 + 64 + 16)
                nc.vector.reciprocal(inverse[:], sums_in[:]).then_inc(inverse_made, 1)

            def divide(g, p):
                dve.wait_ge(stored[p], (g - p) * 8 + 16)
                dve.wait_ge(raw_made, g + 2)
                dve.wait_ge(inverse_loaded, g * 64 + 64)
                nc.vector.tensor_tensor(result[p][:], raw[:], inverse_wide[:], ALU.mult).then_inc(divided, 1)

            def group(g, p, plan):
                for u in range(U):
                    for n, use in enumerate(plan):
                        if use[0] == u:
                            m_use(g, p, plan, n)
                    if plan is not FIRST and u == INVERT:
                        invert(g - 1)
                    if plan is not FIRST and u == DIVIDE:
                        divide(g - 1, 1 - p)

            for n in range(len(START)):
                m_use(0, 0, START, n)
            groups(dve, group)
            for n in range(len(END)):
                m_use(NG, 0, END, n)
            invert(NG - 1)
            divide(NG - 1, 1)


def finish(nc, x, attended, mu, wo, wr, wk, wv, ident, out):
    with ExitStack() as ctx:
        def sb(name, shape, dt=F32):
            return ctx.enter_context(nc.sbuf_tensor("c_" + name, shape, dt))

        def sem(name):
            return ctx.enter_context(nc.semaphore("c_" + name))

        a_in = sb("a_in", [P, G, BLK])
        a_half = [sb(f"a_half{s}", [P, G, BLK], F32R) for s in range(2)]
        x1 = [sb(f"x1_{j}", [P, TT, D]) for j in range(NB)]
        xn = sb("xn", [P, TT, D])
        xT = sb("xT", [P, C, 1 + BLK])
        part = [sb(f"part{c}", [P, BLK]) for c in range(3)]
        mixed = [sb(f"mixed{c}", [P, BLK]) for c in range(C)]
        xk = [sb(f"xk{s}", [P, C, BLK], F32R) for s in range(2)]
        xr = [sb(f"xr{s}", [P, C, BLK], F32R) for s in range(2)]
        act_sq = [sb(f"act_sq{o}", [P, BLK]) for o in range(C)]
        kact = [sb(f"kact{s}", [P, C, BLK], F32R) for s in range(2)]
        gate = sb("gate", [P, TT, D])
        final = sb("final", [P, TT, D])
        mus = [sb(f"mu{k}", [P, C]) for k in range(2)]
        rest = [sb(f"rest{k}", [P, C]) for k in range(2)]
        stats = sb("stats", [P, TT, 6])
        moments = sb("moments", [P, TT, 2])
        variance = sb("variance", [P, TT])
        power = sb("power", [P, TT])
        rstd = sb("rstd", [P, TT])
        t_bank = [ctx.enter_context(nc.psum_tensor(f"c_t{k}", [P, BLK], F32)) for k in range(2)]
        a_bank = [ctx.enter_context(nc.psum_tensor(f"c_a{k}", [P, BLK], F32)) for k in range(2)]
        v_bank = [ctx.enter_context(nc.psum_tensor(f"c_v{k}", [P, BLK], F32)) for k in range(4)]
        mu_loaded = sem("mu_loaded")
        rest_made = sem("rest_made")
        a_loaded = sem("a_loaded")
        x_loaded = [sem(f"x_loaded{j}") for j in range(NB)]
        a_high = sem("a_high")
        a_low = sem("a_low")
        o_done = sem("o_done")
        x1_made = sem("x1_made")
        stats_made = sem("stats_made")
        stats_seen = sem("stats_seen")
        moments_made = sem("moments_made")
        variance_made = sem("variance_made")
        power_made = sem("power_made")
        rstd_made = sem("rstd_made")
        normalised = sem("normalised")
        turned = sem("turned")
        t_free = sem("t_free")
        carried = sem("carried")
        part_made = sem("part_made")
        mix_made = sem("mix_made")
        mix_high = sem("mix_high")
        mix_low = sem("mix_low")
        k_done = sem("k_done")
        r_done = sem("r_done")
        v_done = sem("v_done")
        a_free = sem("a_free")
        v_free = sem("v_free")
        relu_made = sem("relu_made")
        square_made = sem("square_made")
        kact_high = sem("kact_high")
        kact_low = sem("kact_low")
        gate_made = sem("gate_made")
        product_made = sem("product_made")
        final_made = sem("final_made")
        stored = sem("stored")
        block = ctx.enter_context(nc.Block())

        @block.sync
        def _(sp):
            def load_a(i, j):
                sp.dma_start(a_in[:], attended[i, :, :, j * BLK:(j + 1) * BLK].rearrange("g p t -> p g t")
                             ).then_inc(a_loaded, 16)

            def load_x(i, j):
                sp.dma_start(x1[j][:], x[i, j * BLK:(j + 1) * BLK, :].rearrange("(t p) c -> p t c", p=P)
                             ).then_inc(x_loaded[j], 16)

            def stage(i, j, after):
                n = NB * i + j
                if after:
                    sp.wait_ge(a_high, n + 2)
                    sp.wait_ge(a_low, n + 2)
                    load_a(*after)
                sp.wait_ge(final_made, n * TT + 2 * TT)
                sp.dma_start(out[i, j * BLK:(j + 1) * BLK, :].rearrange("(t p) c -> p t c", p=P), final[:]
                             ).then_inc(stored, 16)
                if after:
                    load_x(*after)

            for k in range(2):
                sp.dma_start(mus[k][:], mu[k].rearrange("(c p) -> p c", p=P), allow_slow_non_contiguous=True).then_inc(mu_loaded, 16)
            load_a(0, 0)
            load_x(0, 0)
            load_x(0, 1)
            sp.wait_ge(a_high, 1)
            sp.wait_ge(a_low, 1)
            load_a(0, 1)
            with sp.Fori(0, B - 1) as i:
                stage(i, 0, (i + 1, 0))
                stage(i, 1, (i + 1, 1))
            stage(B - 1, 0, None)
            stage(B - 1, 1, None)
            sp.wait_ge(stored, 16 * (NB * B + 1))

        @block.gpsimd
        def _(pool):
            nc.gpsimd.memset(power[:], -0.5).then_inc(power_made, 1)
            pool.wait_ge(power_made, 1)
            with pool.Fori(0, NB * B) as n:
                pool.wait_ge(a_high, n + 1)
                nc.gpsimd.tensor_tensor(a_half[1][:], a_in[:], a_half[0][:].bitcast(F32), ALU.subtract).then_inc(a_low, 1)
                pool.wait_ge(variance_made, n + 1)
                nc.gpsimd.tensor_tensor(rstd[:], variance[:], power[:], ALU.pow).then_inc(rstd_made, 1)

        @block.tensor
        def _(pe):
            def attention_out(n, before):
                pe.wait_ge(a_low, n + 1)
                for tt in range(TT):
                    pe.wait_ge(v_free, n * (2 * TT) + (before + tt + 1))
                    products(nc, v_bank[tt][:], lambda s, c: a_half[s][:, c, tt * P:(tt + 1) * P],
                             lambda s, c: wo[s][:, c, :]).then_inc(o_done, 1)

            def turn(n):
                pe.wait_ge(normalised, n + 1)
                for c in range(C):
                    pe.wait_ge(t_free, n * C + (c + 1))
                    for tt in range(TT):
                        last = nc.tensor.transpose(t_bank[c % 2][:, tt * P:(tt + 1) * P], xn[:, tt, c * P:(c + 1) * P], ident[:])
                    last.then_inc(turned, 1)

            def stage(n, ahead):
                pe.wait_ge(mix_low, n * (2 * C) + C)
                for o in range(C):
                    pe.wait_ge(a_free, n * (C + TT) + (o + 1))
                    products(nc, a_bank[o % 2][:], lambda s, c: wk[s][:, c, o * P:(o + 1) * P],
                             lambda s, c: xk[s][:, c, :]).then_inc(k_done, 1)
                if ahead:
                    attention_out(n + 1, -TT)
                pe.wait_ge(mix_low, n * (2 * C) + 2 * C)
                for tt in range(TT):
                    pe.wait_ge(a_free, n * (C + TT) + (C + tt + 1))
                    products(nc, a_bank[tt % 2][:], lambda s, c: xr[s][:, c, tt * P:(tt + 1) * P],
                             lambda s, c: wr[s][:, c, :]).then_inc(r_done, 1)
                if ahead:
                    turn(n + 1)
                pe.wait_ge(kact_low, n * C + 2 * C)
                for tt in range(TT):
                    pe.wait_ge(v_free, n * (2 * TT) + ((2 if ahead else 1) * TT + tt + 1))
                    products(nc, v_bank[tt][:], lambda s, c: kact[s][:, c, tt * P:(tt + 1) * P],
                             lambda s, c: wv[s][:, c, :]).then_inc(v_done, 1)

            attention_out(0, 0)
            turn(0)
            with pe.Fori(0, NB * B - 1) as n:
                stage(n, True)
            stage(NB * B - 1, False)

        @block.scalar
        def _(act):
            def a_split(n, first=False):
                act.wait_ge(a_loaded, n * 16 + 16)
                if not first:
                    act.wait_ge(o_done, n * TT)
                nc.scalar.activation(a_half[0][:], a_in[:], ACT.Copy).then_inc(a_high, 1)

            def turned_copy(n):
                act.wait_ge(carried, n + 1)
                for c in range(C):
                    act.wait_ge(turned, n * C + (c + 1))
                    nc.scalar.activation(xT[:, c, 1:1 + BLK], t_bank[c % 2][:], ACT.Copy).then_inc(t_free, 1)

            def mix_split(n, k):
                for c in range(C):
                    act.wait_ge(mix_made, n * (2 * C) + (k * C + c + 1))
                    nc.scalar.activation((xk, xr)[k][0][:, c, :], mixed[c][:], ACT.Copy).then_inc(mix_high, 1)

            def square_high(n, o):
                act.wait_ge(square_made, n * C + (o + 1))
                nc.scalar.activation(kact[0][:, o, :], act_sq[o][:], ACT.Copy).then_inc(kact_high, 1)

            def stage(n, ahead):
                if ahead:
                    a_split(n + 1)
                for o in range(C):
                    act.wait_ge(k_done, n * C + (o + 1))
                    act.wait_ge(kact_low, n * C + (o + 1))
                    nc.scalar.activation(act_sq[o][:], a_bank[o % 2][:], ACT.Relu).then_inc(a_free, 1)
                    if o:
                        square_high(n, o - 1)
                square_high(n, C - 1)
                act.wait_ge(final_made, n * TT + TT)
                for tt in range(TT):
                    act.wait_ge(r_done, n * TT + (tt + 1))
                    nc.scalar.activation(gate[:, tt, :], a_bank[tt % 2][:], ACT.Sigmoid).then_inc(a_free, 1)
                if ahead:
                    turned_copy(n + 1)
                    mix_split(n + 1, 0)
                    mix_split(n + 1, 1)

            a_split(0, first=True)
            turned_copy(0)
            mix_split(0, 0)
            mix_split(0, 1)
            with act.Fori(0, NB * B - 1) as n:
                stage(n, True)
            stage(NB * B - 1, False)

        @block.vector
        def _(dve):
            dve.sem_inc(t_free, 2)
            dve.sem_inc(a_free, 2)
            dve.sem_inc(v_free, TT)
            dve.sem_inc(kact_low, C)
            dve.sem_inc(final_made, TT)
            dve.sem_inc(stored, 16)
            dve.wait_ge(mu_loaded, 32)
            for k in range(2):
                nc.vector.tensor_scalar(rest[k][:], mus[k][:], -1.0, 1.0, ALU.mult, ALU.add).then_inc(rest_made, 1)
            nc.vector.memset(xT[:, :, 0:1], 0.0).then_inc(carried, 1)
            dve.wait_ge(rest_made, 2)

            def residual(i, j, before):
                n = NB * i + j
                dve.wait_ge(x_loaded[j], i * 16 + 16)
                for tt in range(TT):
                    dve.wait_ge(o_done, n * TT + (tt + 1))
                    nc.vector.tensor_tensor(x1[j][:, tt, :], v_bank[tt][:], x1[j][:, tt, :], ALU.add).then_inc(v_free, 1)
                for tt in range(TT):
                    dve.wait_ge(v_free, n * (2 * TT) + (TT + before + tt + 1))
                    last = nc.vector.bn_stats(stats[:, tt, :], x1[j][:, tt, :])
                last.then_inc(stats_made, 1)
                dve.wait_ge(stats_made, n + 1)
                dve.sem_inc(stats_seen, 1)
                for tt in range(TT):
                    last = nc.vector.bn_aggr(moments[:, tt, :], stats[:, tt, :])
                last.then_inc(moments_made, 1)
                dve.wait_ge(moments_made, n + 1)
                nc.vector.tensor_scalar(variance[:], moments[:, :, 1], EPS, None, ALU.add).then_inc(variance_made, 1)
                dve.wait_ge(rstd_made, n + 1)
                for tt in range(TT):
                    last = nc.vector.tensor_scalar(xn[:, tt, :], x1[j][:, tt, :], moments[:, tt, 0:1],
                                                   rstd[:, tt:tt + 1], ALU.subtract, ALU.mult)
                last.then_inc(normalised, 1)

            def mix(n, k):
                m = n * (2 * C) + k * C

                def part_of(c):
                    dve.wait_ge(t_free, n * C + (2 + c + 1))
                    if c == 3:
                        dve.wait_ge(mix_made, m + 1)
                    nc.vector.tensor_scalar(part[c % 3][:], xT[:, c, 0:BLK], rest[1 - k][:, c:c + 1], None, ALU.mult
                                            ).then_inc(part_made, 1)

                def whole(c):
                    dve.wait_ge(part_made, m + (c + 1))
                    nc.vector.scalar_tensor_tensor(mixed[c][:], xT[:, c, 1:1 + BLK], mus[1 - k][:, c:c + 1], part[c % 3][:],
                                                   ALU.mult, ALU.add).then_inc(mix_made, 1)

                def low(c):
                    dve.wait_ge(mix_high, m + (c + 1))
                    nc.vector.tensor_tensor((xk, xr)[k][1][:, c, :], mixed[c][:], (xk, xr)[k][0][:, c, :].bitcast(F32),
                                            ALU.subtract).then_inc(mix_low, 1)

                part_of(0)
                for c in range(C):
                    if c + 1 < C:
                        part_of(c + 1)
                    whole(c)
                    if c:
                        low(c - 1)
                low(C - 1)

            def carry(j):
                if j == NB - 1:
                    nc.vector.memset(xT[:, :, 0:1], 0.0).then_inc(carried, 1)
                else:
                    nc.vector.tensor_copy(xT[:, :, 0:1], xT[:, :, BLK:BLK + 1]).then_inc(carried, 1)

            def stage(i, j, ahead):
                n = NB * i + j

                def square(o):
                    dve.wait_ge(a_free, n * (C + TT) + (2 + o + 1))
                    nc.vector.tensor_tensor(act_sq[o][:], act_sq[o][:], act_sq[o][:], ALU.mult).then_inc(square_made, 1)

                def square_low(o):
                    dve.wait_ge(kact_high, n * C + (o + 1))
                    nc.vector.tensor_tensor(kact[1][:, o, :], act_sq[o][:], kact[0][:, o, :].bitcast(F32), ALU.subtract
                                            ).then_inc(kact_low, 1)

                square(0)
                for o in range(1, C):
                    square(o)
                    square_low(o - 1)
                square_low(C - 1)
                if ahead:
                    i1, j1 = ahead
                    residual(i1, j1, -TT)
                    mix(NB * i1 + j1, 0)
                    mix(NB * i1 + j1, 1)
                    carry(j1)
                dve.wait_ge(stored, n * 16 + 16)
                dve.wait_ge(a_free, n * (C + TT) + (2 + C + TT))
                for tt in range(TT):
                    dve.wait_ge(v_done, n * TT + (tt + 1))
                    nc.vector.tensor_tensor(final[:, tt, :], v_bank[tt][:], gate[:, tt, :], ALU.mult).then_inc(v_free, 1)
                for tt in range(TT):
                    dve.wait_ge(v_free, n * (2 * TT) + (TT + (2 if ahead else 1) * TT + tt + 1))
                    nc.vector.tensor_tensor(final[:, tt, :], final[:, tt, :], x1[j][:, tt, :], ALU.add).then_inc(final_made, 1)

            residual(0, 0, 0)
            mix(0, 0)
            mix(0, 1)
            carry(0)
            with dve.Fori(0, B - 1) as i:
                stage(i, 0, (i, 1))
                stage(i, 1, (i + 1, 0))
            stage(B - 1, 0, (B - 1, 1))
            stage(B - 1, 1, None)


def block_program(nc, x, context, mask, wq, wk, wv, wo, wr, wkf, wvf, mu_r, mu_k, out):
    q_half = [nc.dram_tensor(f"q_half{s}", (B, G, P, L), F32) for s in range(2)]
    k_half = [nc.dram_tensor(f"k_half{s}", (B, G, P, L), F32) for s in range(2)]
    v_rows = nc.dram_tensor("v_rows", (B, G, P, KC, P), F32)
    mask_rows = nc.dram_tensor("mask_rows", (NG, L), F32)
    inverse_rows = nc.dram_tensor("inverse_rows", (NG, HG, L), F32)
    attended = nc.dram_tensor("attended", (NG, P, L), F32)
    with ExitStack() as ctx:
        ident = ctx.enter_context(nc.sbuf_tensor("ident", [P, P], F32))
        identity_made = ctx.enter_context(nc.semaphore("identity_made"))
        with ExitStack() as scope:
            w = [[scope.enter_context(nc.sbuf_tensor(f"qkv_w{k}_{s}", [P, C, D], F32R)) for s in range(2)] for k in range(3)]
            prepare_weights(nc, "qkv", [wq, wk, wv], w, ident, identity_made, True, mask, mask_rows.ap())
            project(nc, x, context, w[0], w[1], w[2], ident,
                    [t.ap().rearrange("b g p t -> b p g t") for t in q_half],
                    [t.ap().rearrange("b g p t -> b p g t") for t in k_half], v_rows.ap())

        attend(nc, [t.ap().rearrange("b g p t -> (b g) p t") for t in q_half],
               [t.ap().rearrange("b g p t -> (b g) p t") for t in k_half],
               v_rows.ap().rearrange("b g p c d -> (b g) p c d"), mask_rows.ap(), inverse_rows.ap(), ident,
               attended.ap())

        with ExitStack() as scope:
            w = [[scope.enter_context(nc.sbuf_tensor(f"ork_w{k}_{s}", [P, C, D], F32R)) for s in range(2)] for k in range(4)]
            prepare_weights(nc, "ork", [wo, wr, wkf, wvf], w, ident, identity_made, False)
            finish(nc, x, attended.ap().rearrange("(b g) p t -> b g p t", g=G), (mu_r, mu_k), w[0], w[1], w[2], w[3],
                   ident, out)


_INS = ['x', 'ctx_1024', 'mask_Bx1x1xS2_bf1', 'L0_xattn_Wq', 'L0_xattn_Wk', 'L0_xattn_Wv', 'L0_xattn_Wo',
        'L0_ffn_W_r', 'L0_ffn_W_k', 'L0_ffn_W_v', 'L0_ffn_mu_r', 'L0_ffn_mu_k']


def kernel(**inputs):
    import numpy as _np
    import concourse.bacc as _bacc
    from concourse import mybir as _mybir
    from concourse.bass_utils import run_bass_kernel_spmd as _run

    nc = _bacc.Bacc("TRN2", target_bir_lowering=False, num_devices=1)
    arrays, args = {}, []
    for name in _INS:
        a = _np.ascontiguousarray(inputs[name])
        arrays[f"in_{name}_dram"] = a
        args.append(nc.dram_tensor(f"in_{name}_dram", a.shape, _mybir.dt.from_np(a.dtype), kind="ExternalInput").ap())
    args.append(nc.dram_tensor("out_0_dram", (8, 1024, 512), _mybir.dt.float32, kind="ExternalOutput").ap())
    block_program(nc, *args)
    r = _run(nc, [arrays], core_ids=[0])
    return r.results[0]["out_0_dram"]
```

```python
from contextlib import ExitStack

import concourse.bass as bass
from concourse import mybir
from concourse.alu_op_type import AluOpType as ALU

F32 = mybir.dt.float32
F32R = mybir.dt.float32r
U8 = mybir.dt.uint8
ACT = mybir.ActivationFunctionType

B, L, D = 8, 1024, 512
H, DH = 16, 32
P = 128
C = D // P
BLK = 512
NB = L // BLK
TT = BLK // P
HG = P // DH
G = H // HG
QT = L // P
KC = L // P
NG = B * G
STACK = 3 * DH + 1
EPS = 1e-5
SCALE = float(1.0 / DH ** 0.5)
MASKED = float(2.0 ** 120)


def products(nc, out, stat, mov):
    n = 0
    for c in range(C):
        for s, m in ((1, 0), (0, 1), (0, 0)):
            last = nc.tensor.matmul(out, stat(s, c), mov(m, c), start=n == 0, stop=n == 3 * C - 1)
            n += 1
    return last


def make_identity(nc, ident, made):
    nc.gpsimd.memset(ident[:], 0.0).then_inc(made, 1)
    nc.gpsimd.wait_ge(made, 1)
    nc.gpsimd.affine_select(out=ident[:], in_=ident[:], compare_op=ALU.not_equal, fill=1.0, base=0,
                            pattern=[[-1, P]], channel_multiplier=1).then_inc(made, 1)


def weight_space(nc, ctx, tag, count):
    nat = [ctx.enter_context(nc.sbuf_tensor(f"{tag}_nat{k}", [P, C, D], F32)) for k in range(count)]
    loaded = [ctx.enter_context(nc.semaphore(f"{tag}_loaded{k}")) for k in range(count)]
    return nat, loaded


def load_weights(sp, weights, nat, loaded):
    for k, w in enumerate(weights):
        sp.dma_start(nat[k][:], w.rearrange("(o p) c -> p o c", p=P)).then_inc(loaded[k], 16)


def prepare_weights(nc, tag, weights, nat, loaded, halves, ident, identity_made, started, mask=None, mask_rows=None):
    with ExitStack() as ctx:
        banks = [ctx.enter_context(nc.psum_tensor(f"{tag}_bank{k}", [P, D], F32)) for k in range(4)]
        transposed = ctx.enter_context(nc.semaphore(f"{tag}_transposed"))
        high_made = ctx.enter_context(nc.semaphore(f"{tag}_high"))
        low_made = ctx.enter_context(nc.semaphore(f"{tag}_low"))
        if mask is not None:
            mask_in = ctx.enter_context(nc.sbuf_tensor("mask_in", [B, L], U8))
            mask_row = ctx.enter_context(nc.sbuf_tensor("mask_row", [B, L], F32R))
            mask_loaded = ctx.enter_context(nc.semaphore("mask_loaded"))
            mask_made = ctx.enter_context(nc.semaphore("mask_made"))
            mask_stored = ctx.enter_context(nc.semaphore("mask_stored"))
        block = ctx.enter_context(nc.Block())

        @block.sync
        def _(sp):
            load_weights(sp, weights[started:], nat[started:], loaded[started:])
            if mask is not None:
                sp.dma_start(mask_in[:], mask.rearrange("b x y k -> (b x y) k")).then_inc(mask_loaded, 16)
                sp.wait_ge(mask_made, 1)
                for g in range(G):
                    sp.dma_start(mask_rows.rearrange("(b g) k -> g b k", g=G)[g],
                                 mask_row[:].bitcast(F32)).then_inc(mask_stored, 16)
                sp.wait_ge(mask_stored, 16 * G)

        @block.gpsimd
        def _(pool):
            if mask is not None:
                make_identity(nc, ident, identity_made)

        @block.tensor
        def _(pe):
            pe.wait_ge(identity_made, 2)
            for k in range(len(weights)):
                pe.wait_ge(loaded[k], 16)
                for c in range(C):
                    n = k * C + c
                    if n >= 4:
                        pe.wait_ge(low_made, n - 3)
                    for o in range(C):
                        last = nc.tensor.transpose(banks[n % 4][:, o * P:(o + 1) * P],
                                                   nat[k][:, o, c * P:(c + 1) * P], ident[:])
                    last.then_inc(transposed, 1)

        @block.scalar
        def _(act):
            for k in range(len(weights)):
                for c in range(C):
                    n = k * C + c
                    act.wait_ge(transposed, n + 1)
                    nc.scalar.activation(halves[k][0][:, c, :], banks[n % 4][:], ACT.Copy).then_inc(high_made, 1)

        @block.vector
        def _(dve):
            for k in range(len(weights)):
                for c in range(C):
                    n = k * C + c
                    dve.wait_ge(high_made, n + 1)
                    nc.vector.tensor_tensor(halves[k][1][:, c, :], banks[n % 4][:],
                                            halves[k][0][:, c, :].bitcast(F32), ALU.subtract).then_inc(low_made, 1)
            if mask is not None:
                dve.wait_ge(mask_loaded, 16)
                nc.vector.tensor_scalar(mask_row[:], mask_in[:], MASKED, -MASKED, ALU.mult, ALU.add).then_inc(mask_made, 1)


def project(nc, x, ctx_in, wq, wk, wv, ident, q_half, k_half, v_rows, q_scale=SCALE):
    with ExitStack() as ctx:
        def sb(name, shape, dt=F32):
            return ctx.enter_context(nc.sbuf_tensor("a_" + name, shape, dt))

        def sem(name):
            return ctx.enter_context(nc.semaphore("a_" + name))

        x_in = [sb(f"x_in{j}", [P, TT, D]) for j in range(NB)]
        c_in = [sb(f"c_in{j}", [P, TT, D]) for j in range(NB)]
        xT = [sb(f"xT{s}", [P, C, BLK], F32R) for s in range(2)]
        cT = [sb(f"cT{s}", [P, C, BLK], F32R) for s in range(2)]
        q_out = [sb(f"q_out{s}", [P, C, BLK], F32R) for s in range(2)]
        k_out = [sb(f"k_out{s}", [P, C, BLK], F32R) for s in range(2)]
        v_out = sb("v_out", [P, TT, D])
        stats = sb("stats", [P, TT, 6])
        moments = sb("moments", [P, TT, 2])
        power = sb("power", [P, TT])
        variance = sb("variance", [P, TT])
        rstd = sb("rstd", [P, TT])
        t_bank = [ctx.enter_context(nc.psum_tensor(f"a_t{k}", [P, BLK], F32)) for k in range(2)]
        p_bank = [ctx.enter_context(nc.psum_tensor(f"a_p{k}", [P, BLK], F32)) for k in range(6)]
        x_loaded = [sem(f"x_loaded{j}") for j in range(NB)]
        c_loaded = [sem(f"c_loaded{j}") for j in range(NB)]
        PB = 3 * C
        power_made = sem("power_made")
        stats_made = sem("stats_made")
        stats_seen = sem("stats_seen")
        moments_made = sem("moments_made")
        variance_made = sem("variance_made")
        rstd_made = sem("rstd_made")
        normalised = sem("normalised")
        x_turned = sem("x_turned")
        c_turned = sem("c_turned")
        turned_high = sem("turned_high")
        t_free = sem("t_free")
        projected = sem("projected")
        out_high = sem("out_high")
        bank_free = sem("bank_free")
        q_stored = sem("q_stored")
        k_stored = sem("k_stored")
        v_stored = sem("v_stored")
        block = ctx.enter_context(nc.Block())

        @block.sync
        def _(sp):
            def load_x(i, j):
                sp.dma_start(x_in[j][:], x[i, j * BLK:(j + 1) * BLK, :].rearrange("(t p) c -> p t c", p=P)
                             ).then_inc(x_loaded[j], 16)

            def load_c(i, j):
                sp.dma_start(c_in[j][:], ctx_in[i, j * BLK:(j + 1) * BLK, :].rearrange("(t p) c -> p t c", p=P)
                             ).then_inc(c_loaded[j], 16)

            def store(i, j):
                n = NB * i + j
                for first, out, half, stored in ((0, q_out, q_half, q_stored), (C, k_out, k_half, k_stored)):
                    sp.wait_ge(bank_free, n * PB + (6 + first + C))
                    for s in range(2):
                        sp.dma_start(half[s][i, :, :, j * BLK:(j + 1) * BLK], out[s][:].bitcast(F32)
                                     ).then_inc(stored, 16)
                sp.wait_ge(bank_free, n * PB + (6 + PB))
                for g in range(G):
                    sp.dma_start(v_rows[i, g, :, j * TT:(j + 1) * TT, :], v_out[:, :, g * P:(g + 1) * P]
                                 ).then_inc(v_stored, 16)

            for j in range(NB):
                load_x(0, j)
                load_c(0, j)
            with sp.Fori(0, B - 1) as i:
                for j in range(NB):
                    sp.wait_ge(c_turned, (NB * i + j) * C + C)
                    load_c(i + 1, j)
                    sp.wait_ge(x_turned, (NB * i + j) * C + C)
                    load_x(i + 1, j)
                    store(i, j)
            for j in range(NB):
                store(B - 1, j)
            sp.wait_ge(q_stored, 32 * (NB * B + 1))
            sp.wait_ge(k_stored, 32 * (NB * B + 1))
            sp.wait_ge(v_stored, 16 * G * (NB * B + 1))

        @block.tensor
        def _(pe):
            def turn(src, i, j, before, turned, banks):
                for c in banks:
                    pe.wait_ge(t_free, (NB * i + j) * 2 * C + (before + c + 1))
                    for tt in range(TT):
                        last = nc.tensor.transpose(t_bank[c % 2][:, tt * P:(tt + 1) * P],
                                                   src[:, tt, c * P:(c + 1) * P], ident[:])
                    last.then_inc(turned, 1)

            def turn_x(i, j, banks):
                if 0 in banks:
                    pe.wait_ge(normalised, (NB * i + j) + 1)
                turn(x_in[j], i, j, 0, x_turned, banks)

            def turn_c(i, j, banks):
                if 0 in banks:
                    pe.wait_ge(c_loaded[j], i * 16 + 16)
                turn(c_in[j], i, j, C, c_turned, banks)

            def stage(i, j, ahead):
                n = NB * i + j
                turn_c(i, j, range(2))
                for first, w, src in ((0, wq, xT), (C, wk, cT)):
                    pe.wait_ge(t_free, n * 2 * C + (2 + C + first))
                    for o in range(C):
                        pe.wait_ge(bank_free, n * PB + (first + o + 1))
                        products(nc, p_bank[(first + o) % 6][:], lambda s, c: w[s][:, c, o * P:(o + 1) * P],
                                 lambda s, c: src[s][:, c, :]).then_inc(projected, 1)
                        if first + o == 0:
                            turn_c(i, j, range(2, C))
                if ahead:
                    turn_x(*ahead, range(2))
                for tt in range(TT):
                    pe.wait_ge(bank_free, n * PB + (2 * C + tt + 1))
                    products(nc, p_bank[(2 * C + tt) % 6][:], lambda s, c: cT[s][:, c, tt * P:(tt + 1) * P],
                             lambda s, c: wv[s][:, c, :]).then_inc(projected, 1)
                    if ahead and tt == 0:
                        turn_x(*ahead, range(2, C))

            turn_x(0, 0, range(C))
            with pe.Fori(0, B - 1) as i:
                stage(i, 0, (i, 1))
                stage(i, 1, (i + 1, 0))
            stage(B - 1, 0, (B - 1, 1))
            stage(B - 1, 1, None)

        @block.gpsimd
        def _(pool):
            nc.gpsimd.memset(power[:], -0.5).then_inc(power_made, 1)
            pool.wait_ge(power_made, 1)
            with pool.Fori(0, NB * B) as n:
                pool.wait_ge(variance_made, n + 1)
                nc.gpsimd.tensor_tensor(rstd[:], variance[:], power[:], ALU.pow).then_inc(rstd_made, 1)

        @block.scalar
        def _(act):
            act.sem_inc(q_stored, 32)
            act.sem_inc(k_stored, 32)

            def split_high(i, j, dst, turned):
                for c in range(C):
                    act.wait_ge(turned, (NB * i + j) * C + (c + 1))
                    nc.scalar.activation(dst[:, c, :], t_bank[c % 2][:], ACT.Copy).then_inc(turned_high, 1)

            def stage(i, j, ahead):
                n = NB * i + j
                split_high(i, j, cT[0], c_turned)
                for out, stored, first, scale in ((q_out, q_stored, 0, SCALE), (k_out, k_stored, C, 1.0)):
                    act.wait_ge(stored, n * 32 + 32)
                    for o in range(C):
                        act.wait_ge(projected, n * PB + (first + o + 1))
                        nc.scalar.activation(out[0][:, o, :], p_bank[(first + o) % 6][:], ACT.Copy, scale=scale
                                             ).then_inc(out_high, 1)
                if ahead:
                    split_high(*ahead, xT[0], x_turned)

            split_high(0, 0, xT[0], x_turned)
            with act.Fori(0, B - 1) as i:
                stage(i, 0, (i, 1))
                stage(i, 1, (i + 1, 0))
            stage(B - 1, 0, (B - 1, 1))
            stage(B - 1, 1, None)

        @block.vector
        def _(dve):
            dve.sem_inc(t_free, 2)
            dve.sem_inc(bank_free, 6)
            dve.sem_inc(v_stored, 16 * G)

            def moments_of(i, j):
                n = NB * i + j
                dve.wait_ge(x_loaded[j], i * 16 + 16)
                for tt in range(TT):
                    last = nc.vector.bn_stats(stats[:, tt, :], x_in[j][:, tt, :])
                last.then_inc(stats_made, 1)
                dve.wait_ge(stats_made, n + 1)
                dve.sem_inc(stats_seen, 1)
                for tt in range(TT):
                    last = nc.vector.bn_aggr(moments[:, tt, :], stats[:, tt, :])
                last.then_inc(moments_made, 1)
                dve.wait_ge(moments_made, n + 1)
                nc.vector.tensor_scalar(variance[:], moments[:, :, 1], EPS, None, ALU.add).then_inc(variance_made, 1)

            def normalise(i, j):
                dve.wait_ge(rstd_made, (NB * i + j) + 1)
                for tt in range(TT):
                    last = nc.vector.tensor_scalar(x_in[j][:, tt, :], x_in[j][:, tt, :], moments[:, tt, 0:1],
                                                   rstd[:, tt:tt + 1], ALU.subtract, ALU.mult)
                last.then_inc(normalised, 1)

            def split_low(i, j, before, dst):
                for c in range(C):
                    dve.wait_ge(turned_high, (NB * i + j) * 2 * C + (before + c + 1))
                    nc.vector.tensor_tensor(dst[1][:, c, :], t_bank[c % 2][:], dst[0][:, c, :].bitcast(F32),
                                            ALU.subtract).then_inc(t_free, 1)

            def stage(i, j, ahead):
                n = NB * i + j
                split_low(i, j, C, cT)
                if ahead:
                    moments_of(*ahead)
                for out, first, scale in ((q_out, 0, SCALE), (k_out, C, 1.0)):
                    for o in range(C):
                        dve.wait_ge(out_high, n * 2 * C + (first + o + 1))
                        nc.vector.scalar_tensor_tensor(out[1][:, o, :], p_bank[(first + o) % 6][:], scale,
                                                       out[0][:, o, :].bitcast(F32), ALU.mult, ALU.subtract
                                                       ).then_inc(bank_free, 1)
                    if ahead and first == 0:
                        normalise(*ahead)
                if ahead:
                    split_low(*ahead, 0, xT)
                dve.wait_ge(v_stored, n * (16 * G) + 16 * G)
                for tt in range(TT):
                    dve.wait_ge(projected, n * PB + (2 * C + tt + 1))
                    nc.vector.tensor_copy(v_out[:, tt, :], p_bank[(2 * C + tt) % 6][:]).then_inc(bank_free, 1)

            moments_of(0, 0)
            normalise(0, 0)
            split_low(0, 0, 0, xT)
            with dve.Fori(0, B - 1) as i:
                stage(i, 0, (i, 1))
                stage(i, 1, (i + 1, 0))
            stage(B - 1, 0, (B - 1, 1))
            stage(B - 1, 1, None)

def attend(nc, q_half, k_half, v_rows, mask_rows, inverse_rows, ident, attended, weights, nat, loaded):
    with ExitStack() as ctx:
        def sb(name, shape, dt=F32):
            return ctx.enter_context(nc.sbuf_tensor("b_" + name, shape, dt))

        def sem(name):
            return ctx.enter_context(nc.semaphore("b_" + name))

        U = KC * HG
        TILES = HG * QT
        M0, M1, TURN = 2, 27, 28
        SUMS, INVERT, DIVIDE = 4, 12, TURN
        PARTS = 4
        RING = 4
        ADDED = 6
        A = HG * (ADDED - 1)
        W = HG * L // P
        q_stack = [sb(f"q_stack{p}", [STACK + 2, HG, L], F32R) for p in range(2)]
        k_stack = [sb(f"k_stack{p}", [STACK + 2, HG, L], F32R) for p in range(2)]
        v_in = [sb(f"v_in{p}", [P, KC, P]) for p in range(2)]
        prob = [sb(f"prob{k}", [P, HG, L]) for k in range(RING)]
        acc = [sb(f"acc{p}", [P, HG, L]) for p in range(2)]
        neg_max = sb("neg_max", [P, TILES])
        max_half = [sb(f"max_half{s}", [TILES, P], F32R) for s in range(2)]
        ones_block = sb("ones_block", [P, DH])
        sums = sb("sums", [P, L])
        sums_in = sb("sums_in", [P, W])
        inverse = sb("inverse", [P, W])
        inverse_wide = sb("inverse_wide", [P, L])
        raw = sb("raw", [P, L])
        result = [sb(f"result{p}", [P, L]) for p in range(2)]
        m_bank = [ctx.enter_context(nc.psum_tensor(f"b_m{k}", [P, L], F32)) for k in range(2)]
        score = [ctx.enter_context(nc.psum_tensor(f"b_score{k}", [P, BLK], F32)) for k in range(2)]
        out_bank = ctx.enter_context(nc.psum_tensor("b_out", [P, L], F32))
        ones_made = sem("ones_made")
        ones_set = sem("ones_set")
        block_made = sem("block_made")
        head_loaded = [[sem(f"head_loaded{p}_{h}") for h in range(HG)] for p in range(2)]
        v_loaded = [sem(f"v_loaded{p}") for p in range(2)]
        m_filled = sem("m_filled")
        m_free = sem("m_free")
        max_high = sem("max_high")
        max_set = sem("max_set")
        scored = sem("scored")
        exp_made = sem("exp_made")
        gathered = sem("gathered")
        pool_added = sem("pool_added")
        last_added = sem("last_added")
        sums_moved = sem("sums_moved")
        inverse_made = sem("inverse_made")
        inverse_stored = sem("inverse_stored")
        inverse_loaded = sem("inverse_loaded")
        divided = sem("divided")
        raw_made = sem("raw_made")
        stored = [sem(f"stored{p}") for p in range(2)]
        block = ctx.enter_context(nc.Block())

        def uses(first, last):
            found = []
            for u in range(U):
                if not last and M0 <= u < M1:
                    found += [(u, "tile", n) for n in range(TILES * (u - M0) // (M1 - M0), TILES * (u - M0 + 1) // (M1 - M0))]
                if not first and u in (SUMS, SUMS + 1):
                    found.append((u, "sums", u - SUMS))
                if not last and u == TURN:
                    found.append((u, "turn", 0))
            return found

        START = [(0, "tile", n) for n in range(TILES)] + [(0, "turn", 0)]
        FIRST, MIDDLE, LAST, END = uses(True, False), uses(False, False), uses(False, True), [
            (0, "sums", 0), (0, "sums", 1)]

        def used(g, plan):
            if plan is START:
                return 0
            if plan is FIRST:
                return len(START)
            before = len(START) + len(FIRST) - len(MIDDLE)
            return g * len(MIDDLE) + (before + (len(LAST) - len(MIDDLE) if plan is END else 0))

        def slot(p, plan, n):
            g = 2 - p if plan is MIDDLE else NG - 1 if plan is LAST else NG if plan is END else 0
            return (used(g, plan) + n) % 2

        def read(g, plan, kind):
            return used(g, plan) + (2 + max(n for n, use in enumerate(plan) if use[1] == kind) + 1)

        def filled(g, plan, kind):
            return read(g, plan, kind) - 2

        def groups(eng, group):
            group(0, 0, FIRST)
            with eng.Fori(0, NG // 2 - 1) as i:
                group(i * 2 + 1, 1, MIDDLE)
                group(i * 2 + 2, 0, MIDDLE)
            group(NG - 1, 1, LAST)

        LOADS = 7

        @block.sync
        def _(sp):
            def load_head(g, p, h):
                done = head_loaded[p][h]
                for stack, half, order in ((q_stack, q_half, (0, 0, 1)), (k_stack, k_half, (0, 1, 0))):
                    for r, s in enumerate(order):
                        sp.dma_start(stack[p][r * DH:(r + 1) * DH, h, :].bitcast(F32), half[s][g, h * DH:(h + 1) * DH, :]
                                     ).then_inc(done, 16)
                sp.dma_start(k_stack[p][STACK - 1:STACK, h, :].bitcast(F32), mask_rows[g].rearrange("(a k) -> a k", a=1)
                             ).then_inc(done, 16)

            def load_v(g, p):
                sp.dma_start(v_in[p][:], v_rows[g]).then_inc(v_loaded[p], 16)

            def set_maxima(g, p, plan):
                sp.wait_ge(m_free, read(g if plan is START else g - 1, plan, "turn"))
                for s in range(2):
                    sp.dma_start(q_stack[p][STACK + s:STACK + s + 1, :, :].bitcast(F32), max_half[s][:].bitcast(F32)
                                 ).then_inc(max_set, 16)

            def spread_inverse(g, plan):
                sp.wait_ge(m_free, read(g + 1, plan, "sums"))
                for h in range(HG):
                    sp.dma_start(sums_in[h * DH:(h + 1) * DH, :], sums[h * DH:h * DH + 1, :]).then_inc(sums_moved, 16)
                sp.wait_ge(inverse_made, g + 1)
                sp.dma_start(inverse_rows[g].rearrange("h (a w) -> (h a) w", w=W), inverse[:]).then_inc(inverse_stored, 16)
                sp.wait_ge(inverse_stored, g * 16 + 16)
                sp.wait_ge(divided, g + 1)
                for h in range(HG):
                    sp.dma_start(inverse_wide[h * DH:(h + 1) * DH, :],
                                 inverse_rows[g, h:h + 1, :].broadcast_to([DH, L])).then_inc(inverse_loaded, 16)

            def store(g, p):
                sp.wait_ge(divided, g + 2)
                sp.dma_start(attended[g], result[p][:]).then_inc(stored[p], 16)

            def group(g, p, plan):
                if plan is not FIRST:
                    if plan is MIDDLE:
                        for h in range(HG):
                            sp.wait_ge(scored, g * (2 * U) - 2 * (HG - 1 - h))
                            load_head(g + 1, 1 - p, h)
                        sp.wait_ge(gathered, g * (PARTS * KC) + PARTS * RING)
                        load_v(g + 1, 1 - p)
                    spread_inverse(g - 1, plan)
                if plan is not LAST:
                    set_maxima(g + 1, 1 - p, plan)
                if plan is not FIRST:
                    store(g - 1, 1 - p)

            sp.wait_ge(ones_made, 1)
            for p in range(2):
                for stack, first, rows in ((q_stack, STACK - 1, 1), (k_stack, STACK, 2)):
                    sp.dma_start(stack[p][first:first + rows, :, :].bitcast(F32),
                                 prob[0][0:rows, :, :]).then_inc(ones_set, 16)
            for p in range(2):
                for h in range(HG):
                    load_head(p, p, h)
                load_v(p, p)
            load_weights(sp, weights, nat, loaded)
            set_maxima(0, 0, START)
            groups(sp, group)
            spread_inverse(NG - 1, END)
            store(NG - 1, 1)
            for p in range(2):
                sp.wait_ge(stored[p], 16 * (NG // 2 + 1))

        @block.tensor
        def _(pe):
            def unit(g, p, u, half):
                if u == 0 and half == 0:
                    pe.wait_ge(max_set, g * 32 + 32)
                h, kc = u % HG, u // HG
                nc.tensor.matmul(score[half][:], k_stack[p][:, h, kc * P:(kc + 1) * P],
                                 q_stack[p][:, h, half * BLK:(half + 1) * BLK], start=True, stop=True).then_inc(scored, 1)

            def gather(g, p, kc, part):
                if kc == 0 and part == 0:
                    pe.wait_ge(raw_made, g + 1)
                    pe.wait_ge(v_loaded[p], (g - p) * 8 + 16)
                pe.wait_ge(exp_made, g * (2 * U) + (2 * (kc * HG + HG) + (part * 2 // PARTS) - 1))
                at = slice(part * L // PARTS, (part + 1) * L // PARTS)
                for h in range(HG):
                    last = nc.tensor.matmul(out_bank[h * DH:(h + 1) * DH, at],
                                            v_in[p][:, kc, h * DH:(h + 1) * DH], prob[kc % RING][:, h, at],
                                            tile_position=(0, h * DH),
                                            start=kc == 0 and part % 2 == 0,
                                            stop=kc == KC - 1 and part % 2 == 1)
                last.then_inc(gathered, 1)

            def m_use(g, p, plan, n):
                _, kind, k = plan[n]
                bank = m_bank[slot(p, plan, n)]
                pe.wait_ge(m_free, used(g, plan) + (n + 1))
                if kind == "tile":
                    after = (g, p) if plan is START else (g + 1, 1 - p)
                    h, qt = k // QT, k % QT
                    if qt == 0:
                        pe.wait_ge(head_loaded[after[1]][h], (after[0] - after[1]) * (8 * LOADS) + 16 * LOADS)
                    for half in range(2):
                        last = nc.tensor.matmul(bank[:, half * BLK:(half + 1) * BLK],
                                                q_stack[after[1]][0:STACK, h, qt * P:(qt + 1) * P],
                                                k_stack[after[1]][0:STACK, h, half * BLK:(half + 1) * BLK], start=True, stop=True)
                elif kind == "turn":
                    pe.wait_ge(m_free, used(g, plan) + (n + 2))
                    last = nc.tensor.transpose(bank[0:TILES, 0:P], neg_max[:], ident[:])
                else:
                    pe.wait_ge(last_added, g * HG)
                    pe.wait_ge(pool_added, (g + 1) * A)
                    for r, part in enumerate((prob[ADDED % RING], acc[1 - p])):
                        for h in range(HG):
                            last = nc.tensor.matmul(bank[h * DH:(h + 1) * DH, 0:BLK], ones_block[:], part[:, h, k * BLK:(k + 1) * BLK],
                                                    start=r == 0, stop=r == 1, tile_position=(0, h * DH))
                last.then_inc(m_filled, 1)

            def group(g, p, plan):
                for u in range(U):
                    here = [n for n, use in enumerate(plan) if use[0] == u]
                    cut = len(here) // 2
                    for half in range(2):
                        pe.wait_ge(exp_made, g * (2 * U) + (2 * u + half + 1))
                        if u + 1 < U:
                            unit(g, p, u + 1, half)
                        elif plan is not LAST:
                            unit(g + 1, 1 - p, 0, half)
                        if half == 0:
                            for n in here[:cut]:
                                m_use(g, p, plan, n)
                            if u > 2 * HG - 1:
                                gather(g, p, u // HG - 1, u % HG)
                            elif u > HG:
                                for part in ((0,), (1,), (2, 3))[u - HG - 1]:
                                    gather(g, p, 0, part)
                            elif u < HG and plan is not FIRST:
                                gather(g - 1, 1 - p, KC - 1, u)
                            for n in here[cut:][:len(here) % 2]:
                                m_use(g, p, plan, n)
                        else:
                            for n in here[cut + len(here) % 2:]:
                                m_use(g, p, plan, n)

            pe.sem_inc(gathered, PARTS * RING)
            pe.wait_ge(block_made, 1)
            pe.wait_ge(ones_set, 64)
            for n in range(len(START)):
                m_use(0, 0, START, n)
            unit(0, 0, 0, 0)
            unit(0, 0, 0, 1)
            groups(pe, group)
            for part in range(PARTS):
                gather(NG - 1, 1, KC - 1, part)
            for n in range(len(END)):
                m_use(NG, 0, END, n)

        @block.gpsimd
        def _(pool):
            nc.gpsimd.memset(prob[0][0:2, :, :], 1.0).then_inc(ones_made, 1)
            nc.gpsimd.memset(ones_block[:], 1.0).then_inc(block_made, 1)
            pool.sem_inc(pool_added, A)

            def group(g, p, plan):
                if plan is not FIRST:
                    pool.wait_ge(m_filled, filled(g - 1, MIDDLE, "sums"))
                for kc in range(1, ADDED):
                    for h in range(HG):
                        pool.wait_ge(exp_made, g * (2 * U) + 2 * (kc * HG + h + 1))
                        if kc > 1:
                            pool.wait_ge(pool_added, (g + 1) * A + (HG * (kc - 2) + h + 1))
                        nc.gpsimd.tensor_tensor(acc[p][:, h, :], prob[0][:, h, :] if kc == 1 else acc[p][:, h, :],
                                                prob[kc % RING][:, h, :], ALU.add).then_inc(pool_added, 1)

            groups(pool, group)

        @block.scalar
        def _(act):
            act.sem_inc(raw_made, 1)
            act.wait_ge(ones_set, 64)

            def maxima_high(g, p, plan):
                act.wait_ge(m_filled, read(g if plan is START else g - 1, plan, "turn") - 2)
                if plan is not START:
                    act.wait_ge(max_set, g * 32)
                nc.scalar.activation(max_half[0][:], m_bank[slot(p, plan, len(plan) - 1)][0:TILES, 0:P], ACT.Copy
                                     ).then_inc(max_high, 1)

            def group(g, p, plan):
                for u in range(U):
                    h, kc = u % HG, u // HG
                    if h == 0:
                        act.wait_ge(gathered, g * (PARTS * KC) + (PARTS * kc + PARTS))
                    if kc >= RING:
                        act.wait_ge(pool_added, (g + 1) * A + (HG * (max(kc - RING, 1) - 1) + h + 1))
                    elif kc + KC - RING < ADDED:
                        act.wait_ge(pool_added, g * A + (HG * (kc + KC - RING - 1) + h + 1))
                    elif plan is not FIRST and h == 0:
                        act.wait_ge(m_filled, filled(g, plan, "sums"))
                    for half in range(2):
                        act.wait_ge(scored, g * (2 * U) + (2 * u + half + 1))
                        nc.scalar.activation(prob[kc % RING][:, h, half * BLK:(half + 1) * BLK], score[half][:], ACT.Exp
                                             ).then_inc(exp_made, 1)
                        if plan is not LAST and (u, half) == (TURN + 1, 0):
                            maxima_high(g + 1, p, plan)
                    if plan is not FIRST and u == HG:
                        act.wait_ge(divided, g)
                        act.wait_ge(gathered, g * (PARTS * KC) + PARTS * RING)
                        nc.scalar.activation(raw[:], out_bank[:], ACT.Copy).then_inc(raw_made, 1)

            maxima_high(0, 0, START)
            groups(act, group)
            act.wait_ge(divided, NG)
            act.wait_ge(gathered, NG * (PARTS * KC) + PARTS * RING)
            nc.scalar.activation(raw[:], out_bank[:], ACT.Copy).then_inc(raw_made, 1)

        @block.vector
        def _(dve):
            dve.sem_inc(m_free, 2)
            dve.sem_inc(divided, 1)
            dve.sem_inc(sums_moved, 16)
            for p in range(2):
                dve.sem_inc(stored[p], 16)

            def m_use(g, p, plan, n):
                _, kind, k = plan[n]
                bank = m_bank[slot(p, plan, n)]
                dve.wait_ge(m_filled, used(g, plan) + (n + 1))
                if kind == "tile":
                    nc.vector.tensor_reduce(neg_max[:, k:k + 1], bank[:], mybir.AxisListType.X, ALU.max, negate=True
                                            ).then_inc(m_free, 1)
                elif kind == "turn":
                    dve.wait_ge(max_high, g + (1 if plan is START else 2))
                    nc.vector.tensor_tensor(max_half[1][:], bank[0:TILES, 0:P], max_half[0][:].bitcast(F32), ALU.subtract
                                            ).then_inc(m_free, 1)
                else:
                    if k == 0:
                        dve.wait_ge(sums_moved, (g - 1) * 64 + 16)
                    nc.vector.tensor_copy(sums[:, k * BLK:(k + 1) * BLK], bank[:, 0:BLK]).then_inc(m_free, 1)

            def add_last(g, heads):
                dve.wait_ge(gathered, g * (PARTS * KC) + (PARTS * RING + PARTS * (ADDED + 1)))
                for h in heads:
                    dve.wait_ge(exp_made, g * (2 * U) + 2 * ((KC - 1) * HG + h + 1))
                    nc.vector.tensor_tensor(prob[ADDED % RING][:, h, :], prob[ADDED % RING][:, h, :], prob[(KC - 1) % RING][:, h, :],
                                            ALU.add).then_inc(last_added, 1)

            def invert(g):
                dve.wait_ge(sums_moved, g * 64 + 64 + 16)
                nc.vector.reciprocal(inverse[:], sums_in[:]).then_inc(inverse_made, 1)

            def divide(g, p):
                dve.wait_ge(stored[p], (g - p) * 8 + 16)
                dve.wait_ge(raw_made, g + 2)
                dve.wait_ge(inverse_loaded, g * 64 + 64)
                nc.vector.tensor_tensor(result[p][:], raw[:], inverse_wide[:], ALU.mult).then_inc(divided, 1)

            def group(g, p, plan):
                if plan is not FIRST:
                    add_last(g - 1, range(HG - 1))
                for u in range(U):
                    for n, use in enumerate(plan):
                        if use[0] == u:
                            m_use(g, p, plan, n)
                    if plan is not FIRST and u == M0:
                        add_last(g - 1, range(HG - 1, HG))
                    if plan is not FIRST and u == INVERT:
                        invert(g - 1)
                    if plan is not FIRST and u == DIVIDE:
                        divide(g - 1, 1 - p)

            for n in range(len(START)):
                m_use(0, 0, START, n)
            groups(dve, group)
            add_last(NG - 1, range(HG))
            for n in range(len(END)):
                m_use(NG, 0, END, n)
            invert(NG - 1)
            divide(NG - 1, 1)


def finish(nc, x, attended, mu, wo, wr, wk, wv, ident, spare, out):
    with ExitStack() as ctx:
        def sb(name, shape, dt=F32):
            return ctx.enter_context(nc.sbuf_tensor("c_" + name, shape, dt))

        def sem(name):
            return ctx.enter_context(nc.semaphore("c_" + name))

        a_in = sb("a_in", [P, G, BLK])
        a_half = [sb(f"a_half{s}", [P, G, BLK], F32R) for s in range(2)]
        x1 = [sb(f"x1_{j}", [P, TT, D]) for j in range(NB)]
        xn = sb("xn", [P, TT, D])
        xT = sb("xT", [P, C, 1 + BLK])
        part = [sb(f"part{c}", [P, BLK]) for c in range(3)]
        mixed = [sb(f"mixed{c}", [P, BLK]) for c in range(C)]
        xk = [sb(f"xk{s}", [P, C, BLK], F32R) for s in range(2)]
        xr = [sb(f"xr{s}", [P, C, BLK], F32R) for s in range(2)]
        act_sq = [sb(f"act_sq{o}", [P, BLK]) for o in range(C)]
        kact = [sb(f"kact{s}", [P, C, BLK], F32R) for s in range(2)]
        gate, final = spare
        mus = [sb(f"mu{k}", [P, C]) for k in range(2)]
        rest = [sb(f"rest{k}", [P, C]) for k in range(2)]
        stats = sb("stats", [P, TT, 6])
        moments = sb("moments", [P, TT, 2])
        variance = sb("variance", [P, TT])
        power = sb("power", [P, TT])
        rstd = sb("rstd", [P, TT])
        t_bank = [ctx.enter_context(nc.psum_tensor(f"c_t{k}", [P, BLK], F32)) for k in range(2)]
        a_bank = [ctx.enter_context(nc.psum_tensor(f"c_a{k}", [P, BLK], F32)) for k in range(2)]
        v_bank = [ctx.enter_context(nc.psum_tensor(f"c_v{k}", [P, BLK], F32)) for k in range(4)]
        mu_loaded = sem("mu_loaded")
        rest_made = sem("rest_made")
        a_loaded = sem("a_loaded")
        x_loaded = [sem(f"x_loaded{j}") for j in range(NB)]
        a_high = sem("a_high")
        a_low = sem("a_low")
        o_done = sem("o_done")
        x1_made = sem("x1_made")
        stats_made = sem("stats_made")
        stats_seen = sem("stats_seen")
        moments_made = sem("moments_made")
        variance_made = sem("variance_made")
        power_made = sem("power_made")
        rstd_made = sem("rstd_made")
        normalised = sem("normalised")
        turned = sem("turned")
        t_free = sem("t_free")
        carried = sem("carried")
        part_made = sem("part_made")
        mix_made = sem("mix_made")
        mix_high = sem("mix_high")
        mix_low = sem("mix_low")
        k_done = sem("k_done")
        r_done = sem("r_done")
        v_done = sem("v_done")
        a_free = sem("a_free")
        v_free = sem("v_free")
        relu_made = sem("relu_made")
        square_made = sem("square_made")
        kact_high = sem("kact_high")
        kact_low = sem("kact_low")
        gate_made = sem("gate_made")
        product_made = sem("product_made")
        final_made = sem("final_made")
        stored = sem("stored")
        block = ctx.enter_context(nc.Block())

        @block.sync
        def _(sp):
            def load_a(i, j):
                sp.dma_start(a_in[:], attended[i, :, :, j * BLK:(j + 1) * BLK].rearrange("g p t -> p g t")
                             ).then_inc(a_loaded, 16)

            def load_x(i, j):
                sp.dma_start(x1[j][:], x[i, j * BLK:(j + 1) * BLK, :].rearrange("(t p) c -> p t c", p=P)
                             ).then_inc(x_loaded[j], 16)

            def stage(i, j, after):
                n = NB * i + j
                if after:
                    sp.wait_ge(a_high, n + 2)
                    sp.wait_ge(a_low, n + 2)
                    load_a(*after)
                sp.wait_ge(final_made, n * TT + 2 * TT)
                sp.dma_start(out[i, j * BLK:(j + 1) * BLK, :].rearrange("(t p) c -> p t c", p=P), final[:]
                             ).then_inc(stored, 16)
                if after:
                    load_x(*after)

            for k in range(2):
                sp.dma_start(mus[k][:], mu[k].rearrange("(c p) -> p c", p=P), allow_slow_non_contiguous=True).then_inc(mu_loaded, 16)
            load_a(0, 0)
            load_x(0, 0)
            load_x(0, 1)
            sp.wait_ge(a_high, 1)
            sp.wait_ge(a_low, 1)
            load_a(0, 1)
            with sp.Fori(0, B - 1) as i:
                stage(i, 0, (i + 1, 0))
                stage(i, 1, (i + 1, 1))
            stage(B - 1, 0, None)
            stage(B - 1, 1, None)
            sp.wait_ge(stored, 16 * (NB * B + 1))

        @block.gpsimd
        def _(pool):
            nc.gpsimd.memset(power[:], -0.5).then_inc(power_made, 1)
            pool.wait_ge(power_made, 1)
            with pool.Fori(0, NB * B) as n:
                pool.wait_ge(a_high, n + 1)
                nc.gpsimd.tensor_tensor(a_half[1][:], a_in[:], a_half[0][:].bitcast(F32), ALU.subtract).then_inc(a_low, 1)
                pool.wait_ge(variance_made, n + 1)
                nc.gpsimd.tensor_tensor(rstd[:], variance[:], power[:], ALU.pow).then_inc(rstd_made, 1)

        @block.tensor
        def _(pe):
            def attention_out(n, before):
                pe.wait_ge(a_low, n + 1)
                for tt in range(TT):
                    pe.wait_ge(v_free, n * (2 * TT) + (before + tt + 1))
                    products(nc, v_bank[tt][:], lambda s, c: a_half[s][:, c, tt * P:(tt + 1) * P],
                             lambda s, c: wo[s][:, c, :]).then_inc(o_done, 1)

            def turn(n):
                pe.wait_ge(normalised, n + 1)
                for c in range(C):
                    pe.wait_ge(t_free, n * C + (c + 1))
                    for tt in range(TT):
                        last = nc.tensor.transpose(t_bank[c % 2][:, tt * P:(tt + 1) * P], xn[:, tt, c * P:(c + 1) * P], ident[:])
                    last.then_inc(turned, 1)

            def stage(n, ahead):
                pe.wait_ge(mix_low, n * (2 * C) + C)
                for o in range(C):
                    pe.wait_ge(a_free, n * (C + TT) + (o + 1))
                    products(nc, a_bank[o % 2][:], lambda s, c: wk[s][:, c, o * P:(o + 1) * P],
                             lambda s, c: xk[s][:, c, :]).then_inc(k_done, 1)
                if ahead:
                    attention_out(n + 1, -TT)
                pe.wait_ge(mix_low, n * (2 * C) + 2 * C)
                for tt in range(TT):
                    pe.wait_ge(a_free, n * (C + TT) + (C + tt + 1))
                    products(nc, a_bank[tt % 2][:], lambda s, c: xr[s][:, c, tt * P:(tt + 1) * P],
                             lambda s, c: wr[s][:, c, :]).then_inc(r_done, 1)
                if ahead:
                    turn(n + 1)
                pe.wait_ge(kact_low, n * C + 2 * C)
                for tt in range(TT):
                    pe.wait_ge(v_free, n * (2 * TT) + ((2 if ahead else 1) * TT + tt + 1))
                    products(nc, v_bank[tt][:], lambda s, c: kact[s][:, c, tt * P:(tt + 1) * P],
                             lambda s, c: wv[s][:, c, :]).then_inc(v_done, 1)

            attention_out(0, 0)
            turn(0)
            with pe.Fori(0, NB * B - 1) as n:
                stage(n, True)
            stage(NB * B - 1, False)

        @block.scalar
        def _(act):
            def a_split(n, first=False):
                act.wait_ge(a_loaded, n * 16 + 16)
                if not first:
                    act.wait_ge(o_done, n * TT)
                nc.scalar.activation(a_half[0][:], a_in[:], ACT.Copy).then_inc(a_high, 1)

            def turned_copy(n):
                act.wait_ge(carried, n + 1)
                for c in range(C):
                    act.wait_ge(turned, n * C + (c + 1))
                    nc.scalar.activation(xT[:, c, 1:1 + BLK], t_bank[c % 2][:], ACT.Copy).then_inc(t_free, 1)

            def mix_split(n, k):
                for c in range(C):
                    act.wait_ge(mix_made, n * (2 * C) + (k * C + c + 1))
                    nc.scalar.activation((xk, xr)[k][0][:, c, :], mixed[c][:], ACT.Copy).then_inc(mix_high, 1)

            def square_high(n, o):
                act.wait_ge(square_made, n * C + (o + 1))
                nc.scalar.activation(kact[0][:, o, :], act_sq[o][:], ACT.Copy).then_inc(kact_high, 1)

            def stage(n, ahead):
                if ahead:
                    a_split(n + 1)
                for o in range(C):
                    act.wait_ge(k_done, n * C + (o + 1))
                    act.wait_ge(kact_low, n * C + (o + 1))
                    nc.scalar.activation(act_sq[o][:], a_bank[o % 2][:], ACT.Relu).then_inc(a_free, 1)
                    if o:
                        square_high(n, o - 1)
                square_high(n, C - 1)
                act.wait_ge(final_made, n * TT + TT)
                for tt in range(TT):
                    act.wait_ge(r_done, n * TT + (tt + 1))
                    nc.scalar.activation(gate[:, tt, :], a_bank[tt % 2][:], ACT.Sigmoid).then_inc(a_free, 1)
                if ahead:
                    turned_copy(n + 1)
                    mix_split(n + 1, 0)
                    mix_split(n + 1, 1)

            a_split(0, first=True)
            turned_copy(0)
            mix_split(0, 0)
            mix_split(0, 1)
            with act.Fori(0, NB * B - 1) as n:
                stage(n, True)
            stage(NB * B - 1, False)

        @block.vector
        def _(dve):
            dve.sem_inc(t_free, 2)
            dve.sem_inc(a_free, 2)
            dve.sem_inc(v_free, TT)
            dve.sem_inc(kact_low, C)
            dve.sem_inc(final_made, TT)
            dve.sem_inc(stored, 16)
            dve.wait_ge(mu_loaded, 32)
            for k in range(2):
                nc.vector.tensor_scalar(rest[k][:], mus[k][:], -1.0, 1.0, ALU.mult, ALU.add).then_inc(rest_made, 1)
            nc.vector.memset(xT[:, :, 0:1], 0.0).then_inc(carried, 1)
            dve.wait_ge(rest_made, 2)

            def residual(i, j, before):
                n = NB * i + j
                dve.wait_ge(x_loaded[j], i * 16 + 16)
                for tt in range(TT):
                    dve.wait_ge(o_done, n * TT + (tt + 1))
                    nc.vector.tensor_tensor(x1[j][:, tt, :], v_bank[tt][:], x1[j][:, tt, :], ALU.add).then_inc(v_free, 1)
                for tt in range(TT):
                    dve.wait_ge(v_free, n * (2 * TT) + (TT + before + tt + 1))
                    last = nc.vector.bn_stats(stats[:, tt, :], x1[j][:, tt, :])
                last.then_inc(stats_made, 1)
                dve.wait_ge(stats_made, n + 1)
                dve.sem_inc(stats_seen, 1)
                for tt in range(TT):
                    last = nc.vector.bn_aggr(moments[:, tt, :], stats[:, tt, :])
                last.then_inc(moments_made, 1)
                dve.wait_ge(moments_made, n + 1)
                nc.vector.tensor_scalar(variance[:], moments[:, :, 1], EPS, None, ALU.add).then_inc(variance_made, 1)
                dve.wait_ge(rstd_made, n + 1)
                for tt in range(TT):
                    last = nc.vector.tensor_scalar(xn[:, tt, :], x1[j][:, tt, :], moments[:, tt, 0:1],
                                                   rstd[:, tt:tt + 1], ALU.subtract, ALU.mult)
                last.then_inc(normalised, 1)

            def mix(n, k):
                m = n * (2 * C) + k * C

                def part_of(c):
                    dve.wait_ge(t_free, n * C + (2 + c + 1))
                    if c == 3:
                        dve.wait_ge(mix_made, m + 1)
                    nc.vector.tensor_scalar(part[c % 3][:], xT[:, c, 0:BLK], rest[1 - k][:, c:c + 1], None, ALU.mult
                                            ).then_inc(part_made, 1)

                def whole(c):
                    dve.wait_ge(part_made, m + (c + 1))
                    nc.vector.scalar_tensor_tensor(mixed[c][:], xT[:, c, 1:1 + BLK], mus[1 - k][:, c:c + 1], part[c % 3][:],
                                                   ALU.mult, ALU.add).then_inc(mix_made, 1)

                def low(c):
                    dve.wait_ge(mix_high, m + (c + 1))
                    nc.vector.tensor_tensor((xk, xr)[k][1][:, c, :], mixed[c][:], (xk, xr)[k][0][:, c, :].bitcast(F32),
                                            ALU.subtract).then_inc(mix_low, 1)

                part_of(0)
                for c in range(C):
                    if c + 1 < C:
                        part_of(c + 1)
                    whole(c)
                    if c:
                        low(c - 1)
                low(C - 1)

            def carry(j):
                if j == NB - 1:
                    nc.vector.memset(xT[:, :, 0:1], 0.0).then_inc(carried, 1)
                else:
                    nc.vector.tensor_copy(xT[:, :, 0:1], xT[:, :, BLK:BLK + 1]).then_inc(carried, 1)

            def stage(i, j, ahead):
                n = NB * i + j

                def square(o):
                    dve.wait_ge(a_free, n * (C + TT) + (2 + o + 1))
                    nc.vector.tensor_tensor(act_sq[o][:], act_sq[o][:], act_sq[o][:], ALU.mult).then_inc(square_made, 1)

                def square_low(o):
                    dve.wait_ge(kact_high, n * C + (o + 1))
                    nc.vector.tensor_tensor(kact[1][:, o, :], act_sq[o][:], kact[0][:, o, :].bitcast(F32), ALU.subtract
                                            ).then_inc(kact_low, 1)

                square(0)
                for o in range(1, C):
                    square(o)
                    square_low(o - 1)
                square_low(C - 1)
                if ahead:
                    i1, j1 = ahead
                    residual(i1, j1, -TT)
                    mix(NB * i1 + j1, 0)
                    mix(NB * i1 + j1, 1)
                    carry(j1)
                dve.wait_ge(stored, n * 16 + 16)
                dve.wait_ge(a_free, n * (C + TT) + (2 + C + TT))
                for tt in range(TT):
                    dve.wait_ge(v_done, n * TT + (tt + 1))
                    nc.vector.tensor_tensor(final[:, tt, :], v_bank[tt][:], gate[:, tt, :], ALU.mult).then_inc(v_free, 1)
                for tt in range(TT):
                    dve.wait_ge(v_free, n * (2 * TT) + (TT + (2 if ahead else 1) * TT + tt + 1))
                    nc.vector.tensor_tensor(final[:, tt, :], final[:, tt, :], x1[j][:, tt, :], ALU.add).then_inc(final_made, 1)

            residual(0, 0, 0)
            mix(0, 0)
            mix(0, 1)
            carry(0)
            with dve.Fori(0, B - 1) as i:
                stage(i, 0, (i, 1))
                stage(i, 1, (i + 1, 0))
            stage(B - 1, 0, (B - 1, 1))
            stage(B - 1, 1, None)


def block_program(nc, x, context, mask, wq, wk, wv, wo, wr, wkf, wvf, mu_r, mu_k, out):
    q_half = [nc.dram_tensor(f"q_half{s}", (B, G, P, L), F32) for s in range(2)]
    k_half = [nc.dram_tensor(f"k_half{s}", (B, G, P, L), F32) for s in range(2)]
    v_rows = nc.dram_tensor("v_rows", (B, G, P, KC, P), F32)
    mask_rows = nc.dram_tensor("mask_rows", (NG, L), F32)
    inverse_rows = nc.dram_tensor("inverse_rows", (NG, HG, L), F32)
    attended = nc.dram_tensor("attended", (NG, P, L), F32)
    with ExitStack() as ctx:
        ident = ctx.enter_context(nc.sbuf_tensor("ident", [P, P], F32))
        identity_made = ctx.enter_context(nc.semaphore("identity_made"))
        with ExitStack() as scope:
            w = [[scope.enter_context(nc.sbuf_tensor(f"qkv_w{k}_{s}", [P, C, D], F32R)) for s in range(2)] for k in range(3)]
            with ExitStack() as space:
                nat, loaded = weight_space(nc, space, "qkv", 3)
                prepare_weights(nc, "qkv", [wq, wk, wv], nat, loaded, w, ident, identity_made, 0, mask, mask_rows.ap())
            project(nc, x, context, w[0], w[1], w[2], ident,
                    [t.ap().rearrange("b g p t -> b p g t") for t in q_half],
                    [t.ap().rearrange("b g p t -> b p g t") for t in k_half], v_rows.ap())

        with ExitStack() as scope:
            later = [wo, wr, wkf, wvf]
            early = len(later) // 2
            nat, loaded = weight_space(nc, scope, "o", early)
            attend(nc, [t.ap().rearrange("b g p t -> (b g) p t") for t in q_half],
                   [t.ap().rearrange("b g p t -> (b g) p t") for t in k_half],
                   v_rows.ap().rearrange("b g p c d -> (b g) p c d"), mask_rows.ap(), inverse_rows.ap(), ident,
                   attended.ap(), later[:early], nat, loaded)
            w = [[scope.enter_context(nc.sbuf_tensor(f"ork_w{k}_{s}", [P, C, D], F32R)) for s in range(2)]
                 for k in range(len(later))]
            with ExitStack() as space:
                nat1, loaded1 = weight_space(nc, space, "k", len(later) - early)
                prepare_weights(nc, "ork", later, nat + nat1, loaded + loaded1, w, ident, identity_made, early)
            finish(nc, x, attended.ap().rearrange("(b g) p t -> b g p t", g=G), (mu_r, mu_k), w[0], w[1], w[2], w[3],
                   ident, nat, out)


_INS = ['x', 'ctx_1024', 'mask_Bx1x1xS2_bf1', 'L0_xattn_Wq', 'L0_xattn_Wk', 'L0_xattn_Wv', 'L0_xattn_Wo',
        'L0_ffn_W_r', 'L0_ffn_W_k', 'L0_ffn_W_v', 'L0_ffn_mu_r', 'L0_ffn_mu_k']


def kernel(**inputs):
    import numpy as _np
    import concourse.bacc as _bacc
    from concourse import mybir as _mybir
    from concourse.bass_utils import run_bass_kernel_spmd as _run

    nc = _bacc.Bacc("TRN2", target_bir_lowering=False, num_devices=1)
    arrays, args = {}, []
    for name in _INS:
        a = _np.ascontiguousarray(inputs[name])
        arrays[f"in_{name}_dram"] = a
        args.append(nc.dram_tensor(f"in_{name}_dram", a.shape, _mybir.dt.from_np(a.dtype), kind="ExternalInput").ap())
    args.append(nc.dram_tensor("out_0_dram", (8, 1024, 512), _mybir.dt.float32, kind="ExternalOutput").ap())
    block_program(nc, *args)
    r = _run(nc, [arrays], core_ids=[0])
    return r.results[0]["out_0_dram"]
```
